# Optimizing a Trainium2 kernel written in Bass

```python
import numpy as np
import jax
import jax.numpy as jnp

def _softmax(x, axis=-1):
    return jax.nn.softmax(x, axis=axis)

def _gelu(x):
    return jax.nn.gelu(x, approximate=True)

def _silu(x):
    return jax.nn.silu(x)

def _sigmoid(x):
    return jax.nn.sigmoid(x)

def _layernorm(x, axis=-1, eps=1e-05):
    m = jnp.mean(x, axis=axis, keepdims=True)
    v = jnp.var(x, axis=axis, keepdims=True)
    return (x - m) / jnp.sqrt(v + eps)

def _scatter_add(tgt, idx, src, axis=0):
    return tgt.at[idx].add(src)

def _segment_sum(src, seg, n):
    return jax.ops.segment_sum(src, seg, n)
kernel_name = 'mk_seq_preln_d1_jaxref_r4_2e23f5'

def setup_inputs(seed: int=0):
    np.random.seed(seed)
    _w = jnp.asarray

    def _L0_attn_setup():
        import jax, jax.numpy as jnp
        import numpy as np
        B, T, D_MODEL, D_STATE = (8, 512, 256, 64)
        key = jax.random.key(seed)
        ks = jax.random.split(key, 10)

        def lecun(k, shape):
            fan_in = shape[0]
            return jax.random.normal(k, shape, dtype=jnp.float32) / jnp.sqrt(jnp.float32(fan_in))
        return {'x': jax.random.normal(ks[0], (B, T, D_MODEL), dtype=jnp.float32), 'W_in': lecun(ks[1], (D_MODEL, D_STATE)), 'b_in': jnp.zeros((D_STATE,), dtype=jnp.float32), 'W_gate': lecun(ks[2], (D_MODEL, D_MODEL)), 'b_gate': jnp.zeros((D_MODEL,), dtype=jnp.float32), 'W_out': lecun(ks[3], (D_MODEL, D_MODEL)), 'b_out': jnp.zeros((D_MODEL,), dtype=jnp.float32), 'A': lecun(ks[4], (D_STATE, D_STATE)) * 0.1, 'Bm': lecun(ks[5], (D_STATE, D_STATE)), 'C': lecun(ks[6], (D_MODEL, D_STATE)), 'D': lecun(ks[7], (D_MODEL, D_STATE))}
    _L0_attn_in = _L0_attn_setup()

    def _L0_ffn_setup():
        import jax, jax.numpy as jnp
        import numpy as np
        B, T, D, E = (4, 256, 256, 8)
        HD = 4 * D
        key = jax.random.key(seed)
        k1, k2, k3, k4 = jax.random.split(key, 4)
        std = 0.5 * D ** (-0.5)
        bound = 3.0 ** 0.5 * std
        x = jax.random.normal(k1, (B, T, D), dtype=jnp.float32)
        router_w = jax.random.normal(k2, (E, D), dtype=jnp.float32) * 0.02
        expert_fc = jax.random.uniform(k3, (E, D, HD), dtype=jnp.float32, minval=-bound, maxval=bound)
        expert_proj = jax.random.normal(k4, (E, D, HD), dtype=jnp.float32) * 0.02
        return {'x': x, 'router_w': router_w, 'expert_fc': expert_fc, 'expert_proj': expert_proj}
    _L0_ffn_in = _L0_ffn_setup()
    _d = {'L0_attn_x': _L0_attn_in['x'], 'L0_attn_W_in': _L0_attn_in['W_in'], 'L0_attn_b_in': _L0_attn_in['b_in'], 'L0_attn_W_gate': _L0_attn_in['W_gate'], 'L0_attn_b_gate': _L0_attn_in['b_gate'], 'L0_attn_W_out': _L0_attn_in['W_out'], 'L0_attn_b_out': _L0_attn_in['b_out'], 'L0_attn_A': _L0_attn_in['A'], 'L0_attn_Bm': _L0_attn_in['Bm'], 'L0_attn_C': _L0_attn_in['C'], 'L0_attn_D': _L0_attn_in['D'], 'L0_ffn_router_w': _L0_ffn_in['router_w'], 'L0_ffn_expert_fc': _L0_ffn_in['expert_fc'], 'L0_ffn_expert_proj': _L0_ffn_in['expert_proj']}
    _x0 = _d['L0_attn_x']
    _d['L0_attn_x'] = jax.random.normal(jax.random.fold_in(jax.random.key(seed), 1), (2, 2048, 256), dtype=_x0.dtype)
    del _x0
    return _d

def reference(L0_attn_x, L0_attn_W_in, L0_attn_b_in, L0_attn_W_gate, L0_attn_b_gate, L0_attn_W_out, L0_attn_b_out, L0_attn_A, L0_attn_Bm, L0_attn_C, L0_attn_D, L0_ffn_router_w, L0_ffn_expert_fc, L0_ffn_expert_proj):

    def _L0_attn_ref(x, W_in, b_in, W_gate, b_gate, W_out, b_out, A, Bm, C, D):
        import jax, jax.numpy as jnp
        import numpy as np
        B, T, D_MODEL, D_STATE = (8, 512, 256, 64)
        u = x @ W_in + b_in
        gate = jax.nn.sigmoid(x @ W_gate + b_gate)
        u_t_first = jnp.swapaxes(u, 0, 1)
        h0 = jnp.zeros((x.shape[0], A.shape[0]), dtype=x.dtype)

        def step(h, u_t):
            h = h @ A + u_t @ Bm
            return (h, h)
        _, hs = jax.lax.scan(step, h0, u_t_first)
        hs = jnp.swapaxes(hs, 0, 1)
        y = jnp.einsum('btn,dn->btd', hs, C) + jnp.einsum('btn,dn->btd', u, D)
        y = y * gate
        return y @ W_out + b_out

    def _L0_ffn_ref(x, router_w, expert_fc, expert_proj):
        import jax, jax.numpy as jnp
        import numpy as np
        B, T, D, E = (4, 256, 256, 8)
        HD = 4 * D
        logits = jnp.einsum('btd,ed->bte', x, router_w)
        probs = jax.nn.softmax(logits, axis=-1)
        expert_ids = jnp.argmax(probs, axis=-1)
        mask = jax.nn.one_hot(expert_ids, E, dtype=x.dtype)
        h = jnp.einsum('btd,edh->ebth', x, expert_fc)
        h = jnp.square(jax.nn.relu(h))
        out_e = jnp.einsum('ebth,edh->ebtd', h, expert_proj)
        output = jnp.einsum('ebtd,bte->btd', out_e, mask)
        return output
    x = L0_attn_x
    x = x + _L0_attn_ref(_layernorm(x, axis=-1), L0_attn_W_in, L0_attn_b_in, L0_attn_W_gate, L0_attn_b_gate, L0_attn_W_out, L0_attn_b_out, L0_attn_A, L0_attn_Bm, L0_attn_C, L0_attn_D)
    x = x + _L0_ffn_ref(_layernorm(x, axis=-1), L0_ffn_router_w, L0_ffn_expert_fc, L0_ffn_expert_proj)
    return x

_drawn_inputs = setup_inputs


def setup_inputs(seed=0):
    import zlib

    import numpy as np

    out = dict(_drawn_inputs(seed))
    spreads = {'L0_attn_b_in': (0.0, 0.1), 'L0_attn_b_gate': (0.0, 0.324), 'L0_attn_b_out': (0.0, 0.1)}
    factors = {}
    for name, (base, spread) in spreads.items():
        noise = np.random.default_rng([zlib.crc32(name.encode()), seed]).standard_normal(out[name].shape)
        drawn = base * np.exp(spread * noise) if base else spread * noise
        out[name] = jnp.asarray(drawn.astype(out[name].dtype))
    for name, factor in factors.items():
        out[name] = (out[name] * factor).astype(out[name].dtype)
    return out
```

```python
from contextlib import ExitStack

import concourse.bass as bass
from concourse import mybir

ALU = mybir.AluOpType
ACT = mybir.ActivationFunctionType
F32 = mybir.dt.float32
F32R = mybir.dt.float32r
I32 = mybir.dt.int32
U32 = mybir.dt.uint32
AX_X = mybir.AxisListType.X
P = 128


def ssm_moe_kernel(nc, x, w_in, b_in, w_gate, b_gate, w_out, b_out, a_mat, ab_t, b_mat, c_t, d_t,
                   router_t, fc, proj, out):
    NB, T, D = x.shape
    S = a_mat.shape[0]
    NE = router_t.shape[1]
    HD = fc.shape[3]
    KC = D // P
    HC = HD // P
    NJ = P
    L = T // NJ
    NR = NB * L
    NTOK = NB * T
    BC = NB * NJ
    ROW = D + 2
    TT = 2 * P
    NT = NTOK // TT + NE - 1
    NSLOT = 2 * (NT + 2)
    WC = KC * HD + HC * D
    EPS = 1e-5
    assert NB == 2 and KC == 2 and S == 64 and L == 16 and HC == 8 and NE == 8 and BC == TT

    x_rows = x.rearrange("b (j i) d -> j b i d", i=L)
    scratch = nc.dram_tensor("x1_rows", (NTOK + 1, ROW), F32, kind="Internal").ap()
    scratch_rows = scratch[0:NTOK, :].rearrange("(b j i) w -> j b i w", b=NB, i=L)

    with ExitStack() as ctx:
        def sem(name):
            return ctx.enter_context(nc.semaphore(name))

        def allocator(stack):
            def sb(name, shape, dt=F32):
                return stack.enter_context(nc.sbuf_tensor(name, shape, dt))
            return sb

        sb = allocator(ctx)
        rows = sb("rows", [P, NB, L, ROW])
        gate = sb("gate", [P, KC, L, BC])
        wraw = sb("wraw", [P, WC])
        wh0 = sb("wh0", [P, WC], F32R)
        wl0 = sb("wl0", [P, WC], F32R)
        ident = sb("ident", [P, P])
        ones = sb("ones", [P, P])
        tri = sb("tri", [P, P])
        eps_s = sb("eps_s", [P, 1])
        zero_row = sb("zero_row", [1, ROW])
        lane = sb("lane", [P, P])
        token = sb("token", [P, L, NB])
        prob = sb("prob", [P, NR, NE])
        pick = sb("pick", [P, NR, NE])
        onehot = sb("onehot", [P, NR, NE])
        count = [sb(f"count{n}", [P, NR, NE]) for n in range(2)]
        rmax = sb("rmax", [P, NR])
        rsum = sb("rsum", [P, NR])
        prefer = sb("prefer", [P, NE])
        tiles_i = sb("tiles_i", [P, NE], I32)
        tiles = sb("tiles", [P, NE])
        ends = [sb(f"ends{n}", [P, NE]) for n in range(2)]
        base = sb("base", [P, NE])
        bounds = sb("bounds", [P, NE + 1], I32)
        pos_i = sb("pos_i", [P, NR], I32)
        lo_i = sb("lo_i", [P, NR], I32)
        hi_i = sb("hi_i", [P, NR], I32)
        lo_f = sb("lo_f", [P, NR])
        hi_f = sb("hi_f", [P, NR])
        ids = sb("ids", [P, NSLOT], U32)
        id_in = sb("id_in", [P, 2], U32)
        id_out = sb("id_out", [P, 2], U32)
        fetched = sb("fetched", [P, 2, ROW])
        xe_h = sb("xe_h", [P, KC, TT], F32R)
        xe_l = sb("xe_l", [P, KC, TT], F32R)
        gate_cols = gate[:, :, :, :].rearrange("p m i c -> p (m i c)")
        relu_s = gate_cols[:, 0:4 * TT].rearrange("p (n c) -> p n c", n=4)
        sq_s = gate_cols[:, 4 * TT:8 * TT].rearrange("p (n c) -> p n c", n=4)
        kept = gate_cols[:, 8 * TT:12 * TT].rearrange("p (n h d) -> p n h d", n=2, h=2)
        result = gate_cols[:, 12 * TT:14 * TT].rearrange("p (h d) -> p h d", h=2)
        xe = gate_cols[:, 14 * TT:16 * TT].rearrange("p (h d) -> p h d", h=2)
        slot_v = gate_cols[:, 0:NR * NSLOT].rearrange("p (r s) -> p r s", r=NR)

        mixer = ExitStack()
        sb = allocator(mixer)
        hu = sb("hu", [P, L, BC])
        xn = sb("xn", [P, 2, NB, D])
        xt_h = sb("xt_h", [P, 2, KC, BC], F32R)
        xt_l = sb("xt_l", [P, 2, KC, BC], F32R)
        x2t = sb("x2t", [P, 2, KC, BC])
        u_rows = sb("u_rows", [S, 2, BC])
        yg = sb("yg", [P, 2, KC, BC])
        w_in_s = sb("w_in_s", [P, KC, 2 * S])
        w_in_h = sb("w_in_h", [P, KC, 2 * S], F32R)
        w_in_l = sb("w_in_l", [P, KC, 2 * S], F32R)
        w_gate_s = sb("w_gate_s", [P, KC, D])
        w_gate_h = sb("w_gate_h", [P, KC, D], F32R)
        w_gate_l = sb("w_gate_l", [P, KC, D], F32R)
        w_out_s = sb("w_out_s", [P, KC, D])
        router_s = sb("router_s", [P, KC, NE])
        b_in_s = sb("b_in_s", [P, 1])
        b_gate_s = sb("b_gate_s", [P, KC])
        b_out_s = sb("b_out_s", [P, D])
        ab_t_s = sb("ab_t_s", [S, 2 * S])
        c_t_s = sb("c_t_s", [S, D])
        d_t_s = sb("d_t_s", [P, D])
        ycat = sb("ycat", [P, D])
        step_w = sb("step_w", [P, S])
        powers = sb("powers", [S, L + 1, S])
        pow_t = sb("pow_t", [S, 4, S])
        carry_w = sb("carry_w", [S, 10, S])
        carry_t = sb("carry_t", [S, 5, S])
        chunk_w = sb("chunk_w", [S, L, S])
        stats = sb("stats", [P, L, NB, 6])
        mean_sum = sb("mean_sum", [P, L, NB])
        mean_dif = sb("mean_dif", [P, L, NB])
        var_sum = sb("var_sum", [P, L, NB])
        neg_mean = sb("neg_mean", [P, L, NB])
        var = sb("var", [P, L, NB])
        std = sb("std", [P, L, NB])
        rstd = sb("rstd", [P, L, NB])
        sums_t = sb("sums_t", [P, NB, S])
        carry = sb("carry", [S, 2, NB, NJ])
        stats2 = sb("stats2", [P, 2, NB, 6])
        mv2 = sb("mv2", [P, 2, NB, 2])
        std2 = sb("std2", [P, 2, NB])
        mixer.close()

        sb = allocator(ctx)
        hid_h = sb("hid_h", [P, HC, TT], F32R)
        hid_l = sb("hid_l", [P, HC, TT], F32R)
        wh1 = sb("wh1", [P, WC], F32R)
        wl1 = sb("wl1", [P, WC], F32R)
        wh, wl = [wh0, wh1], [wl0, wl1]
        lo_hot = wh1[:, 0:NR * P].rearrange("p (r c) -> p r c", r=NR)
        slot_r = wl1[:, 0:NR * NSLOT].rearrange("p (r s) -> p r s", r=NR)

        bank = [ctx.enter_context(nc.psum_tensor(f"bank{n}", [P, 512], F32)) for n in range(6)]
        bank67 = ctx.enter_context(nc.psum_tensor("bank67", [P, 2, 512], F32))

        s_ab = sem("s_ab")
        s_x = [sem(f"s_xq{n}") for n in range(4)]
        s_wl = sem("s_wl")
        s_rawf = sem("s_rawf")
        s_rawp = sem("s_rawp")
        s_const = sem("s_const")
        s_split = sem("s_split")
        s_pmm = sem("s_pmm")
        s_pcp = sem("s_pcp")
        s_yc = sem("s_yc")
        s_ycs = sem("s_ycs")
        s_bn0 = sem("s_bn0")
        s_stat = sem("s_stat")
        s_std = sem("s_std")
        s_xn = sem("s_xn")
        s_xt = sem("s_xt")
        s_xth = sem("s_xth")
        s_xtl = sem("s_xtl")
        s_u = sem("s_u")
        s_us = sem("s_us")
        s_g = sem("s_g")
        s_gs = sem("s_gs")
        s_e = sem("s_e")
        s_ecp = sem("s_ecp")
        s_cmm = sem("s_cmm")
        s_ccp = sem("s_ccp")
        s_bias = sem("s_bias")
        s_h = sem("s_h")
        s_hs0 = sem("s_hs0")
        s_hs1 = sem("s_hs1")
        s_y = sem("s_y")
        s_yg = sem("s_yg")
        s_o = sem("s_o")
        s_x1 = sem("s_x1")
        s_bn = sem("s_bn")
        s_mv = sem("s_mv")
        s_nm = sem("s_nm")
        s_std2 = sem("s_std2")
        s_rc = sem("s_rc")
        s_xn2 = sem("s_xn2")
        s_xt2 = sem("s_xt2")
        s_x2s = sem("s_x2s")
        s_lg = sem("s_lg")
        s_st = sem("s_st")
        s_rt = sem("s_rt")
        s_exp = sem("s_exp")
        s_cnt = sem("s_cnt")
        s_hot = sem("s_hot")
        s_slot = sem("s_slot")
        s_ids = sem("s_ids")
        s_wsh = sem("s_wsh")
        s_wsp = sem("s_wsp")
        s_wsd = sem("s_wsd")
        s_idc = sem("s_idc")
        s_odc = sem("s_odc")
        s_in = sem("s_in")
        s_xe = sem("s_xe")
        s_xet = sem("s_xet")
        s_xeh = sem("s_xeh")
        s_xel = sem("s_xel")
        s_fc = sem("s_fc")
        s_relu = sem("s_relu")
        s_sqh = sem("s_sqh")
        s_sqs = sem("s_sqs")
        s_sql = sem("s_sql")
        s_pj = sem("s_pj")
        s_res = sem("s_res")
        s_out = sem("s_out")

        s_tick = sem("s_tick")

        block = ctx.enter_context(nc.Block())
        QI = L // 4
        R_COUNT = 15
        NWL = 16 * 13
        HALF = WC // 2

        def wait_apart(engine, *waits):
            for s, value in waits:
                engine.wait_ge(s, value)
            engine.sem_inc(s_tick, 1)

        @block.sync
        def _(sp):
            sp.dma_start(ab_t_s[:], ab_t).then_inc(s_ab, 16)
            sp.dma_start(powers[:, L - 1, :], a_mat).then_inc(s_ab, 16)
            for q in range(4):
                for b in range(NB):
                    sp.dma_start(rows[:, b, q * QI:(q + 1) * QI, 0:D],
                                 x_rows[:, b, q * QI:(q + 1) * QI, :]).then_inc(s_x[q], 16)
            for n in range(2):
                sp.dma_start(w_in_s[:, :, n * S:(n + 1) * S],
                             w_in.rearrange("(k p) s -> p k s", p=P)).then_inc(s_wl, 16)
            sp.dma_start(w_gate_s[:], w_gate.rearrange("(k p) s -> p k s", p=P)).then_inc(s_wl, 16)
            with nc.allow_non_contiguous_dma(reason="bias vectors"):
                for n in range(2):
                    sp.dma_start(b_in_s[n * S:(n + 1) * S, :],
                                 b_in.rearrange("(p o) -> p o", o=1)).then_inc(s_wl, 16)
                sp.dma_start(b_gate_s[:], b_gate.rearrange("(k p) -> p k", p=P)).then_inc(s_wl, 16)
            sp.dma_start(c_t_s[:], c_t).then_inc(s_wl, 16)
            sp.dma_start(d_t_s[S:2 * S, :], d_t).then_inc(s_wl, 16)
            sp.dma_start(step_w[0:S, :], a_mat).then_inc(s_wl, 16)
            sp.dma_start(step_w[S:2 * S, :], b_mat).then_inc(s_wl, 16)
            sp.dma_start(w_out_s[:], w_out.rearrange("(k p) s -> p k s", p=P)).then_inc(s_wl, 16)
            sp.dma_start(router_s[:], router_t.rearrange("(k p) s -> p k s", p=P)).then_inc(s_wl, 16)
            sp.dma_start(b_out_s[:], b_out.rearrange("(o d) -> o d", o=1).to_broadcast([P, D])).then_inc(s_wl, 16)
            sp.dma_start(wraw[:, 0:KC * HD], fc[0].rearrange("p k h -> p (k h)")).then_inc(s_rawf, 16)
            sp.dma_start(wraw[:, KC * HD:], proj[0].rearrange("p k d -> p (k d)")).then_inc(s_rawp, 16)
            for q in range(4):
                sp.wait_ge(s_nm, (q + 1) * QI)
                sp.wait_ge(s_rc, (q + 1) * QI)
                sp.dma_start(scratch_rows[:, :, q * QI:(q + 1) * QI, :],
                             rows[:, :, q * QI:(q + 1) * QI, :]).then_inc(s_st, 16)
            with sp.Fori(0, NE - 1) as e:
                sp.wait_ge(s_wsd, e + 1)
                sp.dma_start(wraw[:, 0:HALF],
                             fc[bass.ds(e + 1, 1)].rearrange("o p k h -> p (o k h)")).then_inc(s_rawf, 16)
                sp.wait_ge(s_wsp, e + 1)
                sp.dma_start(wraw[:, HALF:],
                             proj[bass.ds(e + 1, 1)].rearrange("o p k d -> p (o k d)")).then_inc(s_rawp, 16)

        @block.gpsimd
        def _(pool):
            pool.memset(zero_row[:], 0.0).then_inc(s_const, 1)
            pool.memset(ones[:], 1.0).then_inc(s_const, 1)
            pool.wait_ge(s_const, 2)
            pool.dma_start(scratch[NTOK:NTOK + 1, :], zero_row[:]).then_inc(s_out, 32)
            pool.affine_select(out=ident[:], in_=ones[:], compare_op=ALU.is_equal, fill=0.0, base=0,
                               pattern=[[-1, P]], channel_multiplier=1).then_inc(s_const, 1)
            pool.wait_ge(s_const, 3)
            pool.tensor_copy(powers[:, L, :], ident[0:S, 0:S]).then_inc(s_const, 1)
            pool.memset(eps_s[:], EPS).then_inc(s_const, 1)
            pool.affine_select(out=tri[:], in_=ones[:], compare_op=ALU.is_gt, fill=0.0, base=0,
                               pattern=[[1, P]], channel_multiplier=-1).then_inc(s_const, 1)
            pool.iota(prefer[:], pattern=[[-1, NE]], base=NE, channel_multiplier=0,
                      allow_small_or_imprecise_dtypes=True).then_inc(s_const, 1)
            pool.iota(lane[:], pattern=[[1, P]], base=0, channel_multiplier=0,
                      allow_small_or_imprecise_dtypes=True).then_inc(s_const, 1)
            pool.iota(token[:], pattern=[[1, L], [T, NB]], base=-NTOK, channel_multiplier=L,
                      allow_small_or_imprecise_dtypes=True).then_inc(s_const, 1)

            pool.wait_ge(s_wl, NWL)
            pool.tensor_scalar(w_in_h[:], w_in_s[:], 1.0, 0.0, ALU.mult, ALU.add).then_inc(s_split, 1)
            pool.tensor_scalar(w_gate_h[:], w_gate_s[:], 1.0, 0.0, ALU.mult, ALU.add).then_inc(s_split, 1)
            pool.wait_ge(s_split, 2)
            pool.tensor_tensor(w_in_l[:], w_in_s[:], w_in_h[:].bitcast(F32), ALU.subtract).then_inc(s_split, 1)
            pool.tensor_tensor(w_gate_l[:], w_gate_s[:], w_gate_h[:].bitcast(F32), ALU.subtract).then_inc(s_split, 1)

            def high_weights(par, nth):
                for n, loaded in enumerate((s_rawf, s_rawp)):
                    wait_apart(pool, (loaded, (nth + 1) * 16))
                    c = slice(n * HALF, (n + 1) * HALF)
                    pool.tensor_scalar(wh[par][:, c], wraw[:, c], 1.0, 0.0, ALU.mult, ALU.add).then_inc(s_wsh, 1)

            def low_weights(par, nth):
                pool.wait_ge(s_wsh, (nth + 1) * 2)
                c = slice(HALF, WC)
                pool.tensor_tensor(wl[par][:, c], wraw[:, c], wh[par][:, c].bitcast(F32),
                                   ALU.subtract).then_inc(s_wsp, 1)

            with pool.Fori(0, L) as i:
                pool.wait_ge(s_xn, i + 1)
                for b in range(NB):
                    row = rows[:, b, bass.ds(i, 1), 0:D].rearrange("p o d -> p (o d)")
                    last = pool.tensor_tensor(row, row, b_out_s[:], ALU.add)
                last.then_inc(s_bias, 1)

            high_weights(0, 0)
            low_weights(0, 0)

            pool.wait_ge(s_ids, 1)
            pool.wait_ge(s_st, 16 * 4)
            pool.wait_ge(s_out, 32)

            def fetch(t):
                pool.tensor_copy(id_in[:], ids[:, bass.ds(t * 2, 2)]).then_inc(s_idc, 1)
                wait_apart(pool, (s_idc, t + 1))
                for h in range(2):
                    pool.indirect_dma_start(fetched[:, h, :], None, scratch[:, :],
                                            bass.IndirectOffsetOnAxis(ap=id_in[:, h:h + 1], axis=0)) \
                        .then_inc(s_in, 16)

            def store(t):
                pool.tensor_copy(id_out[:], ids[:, bass.ds(t * 2, 2)]).then_inc(s_odc, 1)
                wait_apart(pool, (s_odc, t + 1), (s_res, t + 2))
                for h in range(2):
                    pool.indirect_dma_start(out[:, :], bass.IndirectOffsetOnAxis(ap=id_out[:, h:h + 1], axis=0),
                                            result[:, h, :], None, bounds_check=NTOK - 1, oob_is_err=False) \
                        .then_inc(s_out, 16)

            fetch(0)
            pool.wait_ge(s_xe, 1)
            fetch(1)

            def expert_tiles(e):
                first = pool.value_load(bounds[0:1, bass.ds(e, 1)], min_val=0, max_val=NT - 1)
                end = pool.value_load(bounds[0:1, bass.ds(e + 1, 1)], min_val=1, max_val=NT)
                return first, end

            def ahead(t):
                pool.wait_ge(s_xe, t + 2)
                fetch(t + 2)

            def behind(t):
                pool.wait_ge(s_out, t * 32 + 32)
                store(t)

            def run_tiles(first, end):
                with pool.Fori(first, end) as t:
                    ahead(t)
                    behind(t)

            def run_expert(par, e):
                first, end = expert_tiles(e)
                pool.wait_ge(s_pj, first + 1)
                high_weights(1 - par, e + 1)
                ahead(first)
                low_weights(1 - par, e + 1)
                behind(first)
                with pool.If(first + 1 < end):
                    run_tiles(first + 1, end)

            with pool.Fori(0, NE // 2 - 1) as q:
                for par in range(2):
                    run_expert(par, q * 2 + par)
            run_expert(0, NE - 2)
            first, end = expert_tiles(NE - 1)
            run_tiles(first, end)
            pool.wait_ge(s_out, end * 32 + 32)

        @block.scalar
        def _(act):
            def copies(n, pairs):
                act.wait_ge(s_pmm, n)
                for dst, src in pairs:
                    last = act.copy(dst, src)
                last.then_inc(s_pcp, 1)

            for n, m in enumerate((1, 2, 4, 8)):
                new = bank[5][0:S, 0:m * S]
                pairs = [(powers[:, L - 2 * m:L - m, :].rearrange("p k s -> p (k s)"), new),
                         (pow_t[:, n, :], bank[2][0:S, 0:S])]
                if m == 8:
                    pairs.append((carry_w[:, 0, :], bank[5][0:S, 0:S]))
                copies(n + 1, pairs)
            copies(5, [(chunk_w[:, 0:8, :].rearrange("p k s -> p (k s)"), bank[0][0:S, :]),
                       (chunk_w[:, 8:16, :].rearrange("p k s -> p (k s)"), bank[1][0:S, :])])
            for r in range(3):
                copies(6 + 2 * r, [(carry_w[:, 3 * r + 1, :], bank[5][0:S, 0:S]),
                                   (carry_t[:, 2 * r, :], bank[2][0:S, 0:S])])
                pairs = [(carry_w[:, 3 * r + 2:3 * r + 4, :].rearrange("p k s -> p (k s)"), bank[5][0:S, 0:2 * S])]
                if r < 2:
                    pairs.append((carry_t[:, 2 * r + 1, :], bank[2][0:S, 0:S]))
                copies(7 + 2 * r, pairs)

            act.wait_ge(s_const, 5)
            act.wait_ge(s_stat, 6)
            act.activation(std[:], var[:], ACT.Sqrt, bias=eps_s[:, 0:1]).then_inc(s_std, 1)
            act.wait_ge(s_wl, NWL)

            def high1(i, par, free):
                act.wait_ge(s_xt, i + 1)
                if free:
                    act.wait_ge(s_g, i - 1)
                act.copy(xt_h[:, par, :, :].rearrange("p k c -> p (k c)"), bank[par][:, :]).then_inc(s_xth, 1)

            def block_a(i, par, free, more=True):
                act.wait_ge(s_u, i + 1)
                if free:
                    act.wait_ge(s_e, i - 1)
                act.activation(u_rows[:, par, :], bank[2][0:S, 0:BC], ACT.Identity, bias=b_in_s[0:S, 0:1])
                act.activation(hu[S:2 * S, bass.ds(i, 1), :].rearrange("p o c -> p (o c)"), bank[2][S:2 * S, 0:BC],
                               ACT.Identity, bias=b_in_s[S:2 * S, 0:1]).then_inc(s_us, 1)
                if more:
                    high1(i + 1, 1 - par, free or par == 1)
                act.wait_ge(s_g, i + 1)
                for m in range(KC):
                    last = act.activation(gate[:, m, bass.ds(i, 1), :].rearrange("p o c -> p (o c)"),
                                          bank[3 + par][:, m * BC:(m + 1) * BC], ACT.Sigmoid,
                                          bias=b_gate_s[:, m:m + 1])
                last.then_inc(s_gs, 1)

            high1(0, 0, False)
            block_a(0, 0, False)
            block_a(1, 1, False)
            with act.Fori(1, L // 2 - 1) as q:
                for par in range(2):
                    block_a(q * 2 + par, par, True)
            block_a(L - 2, 0, True)
            block_a(L - 1, 1, True, more=False)

            def block_b(i, par, upto=4 * L):
                if upto == 4 * L or upto < L - 1:
                    act.wait_ge(s_h, i + 1)
                    act.copy(hu[0:S, bass.ds(i + 1, 1), 0:NJ].rearrange("p o c -> p (o c)"),
                             bank[2][0:S, 0:NJ]).then_inc(s_hs0, 1)
                if upto == 4 * L or 1 <= upto < L + 1:
                    act.wait_ge(s_mv, i)
                    if upto >= 3:
                        act.wait_ge(s_rc, i - 2)
                    act.activation(std2[:, 1 - par, :], mv2[:, 1 - par, :, 1], ACT.Sqrt,
                                   bias=eps_s[:, 0:1]).then_inc(s_std2, 1)
                if upto == 4 * L or 3 <= upto < L + 3:
                    act.wait_ge(s_xt2, i - 2)
                    if upto >= 5:
                        act.wait_ge(s_lg, i - 4)
                    act.copy(x2t[:, 1 - par, :, :].rearrange("p k c -> p (k c)"),
                             bank[1 - par][:, :]).then_inc(s_x2s, 1)

            for i in range(6):
                block_b(i, i % 2, i)
            with act.Fori(3, L // 2 - 1) as q:
                for par in range(2):
                    block_b(q * 2 + par, par)
            for i in range(L - 2, L + 3):
                block_b(i, i % 2, i)

            act.wait_ge(s_rt, 2)
            act.activation(prob[:], prob[:], ACT.Exp).then_inc(s_exp, 1)

            def high_x(t):
                act.wait_ge(s_xet, t + 1)
                act.copy(xe_h[:].rearrange("p k c -> p (k c)"), bank[4][:, :]).then_inc(s_xeh, 1)

            act.wait_ge(s_ids, 1)
            high_x(0)
            with act.Fori(0, NE) as e:
                first = act.value_load(bounds[0:1, bass.ds(e, 1)], min_val=0, max_val=NT - 1)
                end = act.value_load(bounds[0:1, bass.ds(e + 1, 1)], min_val=1, max_val=NT)
                with act.Fori(first, end) as t:
                    def square(c):
                        act.wait_ge(s_relu, t * HC + (c + 1))
                        act.activation(hid_h[:, c, :], relu_s[:, c % 4, :], ACT.Square).then_inc(s_sqh, 1)

                    for c in range(HC):
                        act.wait_ge(s_fc, t * HC + (c + 1))
                        if c >= 4:
                            act.wait_ge(s_sqs, t * HC + (c - 3))
                        else:
                            act.wait_ge(s_xel, t + 1)
                        act.activation(relu_s[:, c % 4, :], bank[c % 4][:, 0:TT], ACT.Relu).then_inc(s_relu, 1)
                        if c >= 1:
                            square(c - 1)
                    square(HC - 1)
                    high_x(t + 1)

        @block.tensor
        def _(pe):
            def three_pass(dst, lhs, rhs, start, stop):
                pe.matmul(dst, lhs[1], rhs[0], start=start, stop=False)
                pe.matmul(dst, lhs[0], rhs[1], start=False, stop=False)
                return pe.matmul(dst, lhs[0], rhs[0], start=False, stop=stop)

            def one(dst, lhs, rhs):
                return pe.matmul(dst, lhs, rhs, start=True, stop=True)

            pe.wait_ge(s_ab, 32)
            at, bt = ab_t_s[:, 0:S], ab_t_s[:, S:2 * S]
            tr = at
            for n, m in enumerate((1, 2, 4, 8)):
                if n:
                    pe.wait_ge(s_pcp, n)
                one(bank[5][0:S, 0:m * S], tr, powers[:, L - m:L, :].rearrange("p k s -> p (k s)"))
                one(bank[2][0:S, 0:S], powers[:, L - m, :], tr).then_inc(s_pmm, 1)
                tr = pow_t[:, n, :]
            pe.wait_ge(s_pcp, 4)
            pe.wait_ge(s_const, 4)
            one(bank[0][0:S, :], bt, powers[:, 1:9, :].rearrange("p k s -> p (k s)"))
            one(bank[1][0:S, :], bt, powers[:, 9:17, :].rearrange("p k s -> p (k s)")).then_inc(s_pmm, 1)
            for r in range(3):
                b1, b2 = carry_w[:, 3 * r, :], carry_w[:, 3 * r + 1, :]
                t2 = carry_t[:, 2 * r, :]
                if r:
                    pe.wait_ge(s_pcp, 5 + 2 * r)
                one(bank[5][0:S, 0:S], tr, b1)
                one(bank[2][0:S, 0:S], b1, tr).then_inc(s_pmm, 1)
                pe.wait_ge(s_pcp, 6 + 2 * r)
                last = one(bank[5][0:S, 0:2 * S], t2, carry_w[:, 3 * r:3 * r + 2, :].rearrange("p k s -> p (k s)"))
                if r < 2:
                    last = one(bank[2][0:S, 0:S], b2, t2)
                    tr = carry_t[:, 2 * r + 1, :]
                last.then_inc(s_pmm, 1)
            pe.wait_ge(s_wl, NWL)
            one(bank[3][:, 0:D], ab_t_s[:], c_t_s[:]).then_inc(s_yc, 1)

            def turn(src, par, done):
                for k in range(KC):
                    for b in range(NB):
                        last = pe.transpose(bank[par][:, k * BC + b * NJ:k * BC + (b + 1) * NJ],
                                            src[:, par, b, k * P:(k + 1) * P], ident[:])
                last.then_inc(done, 1)

            def turn_a(i, par, free):
                pe.wait_ge(s_xn, i + 1)
                if free:
                    pe.wait_ge(s_xtl, i - 1)
                turn(xn, par, s_xt)

            def block_a(i, par, nth):
                pe.wait_ge(s_xtl, i + 1)
                xs = lambda k: (xt_h[:, par, k, :], xt_l[:, par, k, :])
                if nth:
                    pe.wait_ge(s_us, i)
                for k in range(KC):
                    last = three_pass(bank[2][:, 0:BC], (w_in_h[:, k, :], w_in_l[:, k, :]), xs(k), k == 0, k == KC - 1)
                last.then_inc(s_u, 1)
                if nth >= 2:
                    pe.wait_ge(s_gs, i - 1)
                for m in range(KC):
                    for k in range(KC):
                        w = (w_gate_h[:, k, m * P:(m + 1) * P], w_gate_l[:, k, m * P:(m + 1) * P])
                        last = three_pass(bank[3 + par][:, m * BC:(m + 1) * BC], w, xs(k), k == 0, k == KC - 1)
                last.then_inc(s_g, 1)
                pe.wait_ge(s_us, i + 1)
                for b in range(NB):
                    last = pe.matmul(bank67[:, b, 0:S], u_rows[:, par, b * NJ:(b + 1) * NJ],
                                     chunk_w[:, bass.ds(i, 1), :].rearrange("p o s -> p (o s)"),
                                     start=(nth == 0), stop=(nth == L - 1))
                last.then_inc(s_e, 1)

            pe.wait_ge(s_split, 4)
            pe.wait_ge(s_pcp, 11)
            turn_a(0, 0, False)
            turn_a(1, 1, False)
            pe.wait_ge(s_ycs, 2)
            block_a(0, 0, 0)
            turn_a(2, 0, True)
            block_a(1, 1, 1)
            with pe.Fori(1, L // 2 - 1) as q:
                for par in range(2):
                    i = q * 2 + par
                    turn_a(i + 1, 1 - par, True)
                    block_a(i, par, 2)
            turn_a(L - 1, 1, True)
            block_a(L - 2, 0, L - 2)
            block_a(L - 1, 1, L - 1)

            pe.wait_ge(s_ecp, 1)
            for b in range(NB):
                pe.transpose(bank[b][0:S, 0:NJ], sums_t[:, b, :], ident[:]).then_inc(s_cmm, 1)
            for r in range(4):
                terms = range(1, 4 if r < 3 else 2)
                for b in range(NB):
                    pe.wait_ge(s_ccp, r * NB + b + 1)
                    for k in terms:
                        far = k * 4 ** r
                        last = pe.matmul(bank[b][0:S, far:NJ], carry_w[:, 3 * r + k - 1, :],
                                         carry[:, r % 2, b, 0:NJ - far], start=(k == 1), stop=(k == terms[-1]))
                    last.then_inc(s_cmm, 1)

            def block_b(i, par, upto=4 * L):
                live = lambda lo, hi: upto == 4 * L or lo <= upto < hi
                if live(0, L - 1):
                    if upto == 0:
                        pe.wait_ge(s_ccp, 5 * NB)
                    else:
                        pe.wait_ge(s_hs0, i)
                        pe.wait_ge(s_hs1, i)
                    for b, dst in enumerate((bank[2][0:S, 0:NJ], bank67[0:S, 1, 0:NJ])):
                        last = one(dst, step_w[:], hu[:, bass.ds(i, 1), b * NJ:(b + 1) * NJ]
                                   .rearrange("p o c -> p (o c)"))
                    last.then_inc(s_h, 1)
                if live(0, L):
                    if upto == L - 1:
                        pe.wait_ge(s_hs0, i)
                        pe.wait_ge(s_hs1, i)
                    if upto >= 2:
                        pe.wait_ge(s_yg, i - 1)
                    for m in range(KC):
                        last = one(bank[3 + par][:, m * BC:(m + 1) * BC], ycat[:, m * P:(m + 1) * P],
                                   hu[:, bass.ds(i, 1), :].rearrange("p o c -> p (o c)"))
                    last.then_inc(s_y, 1)
                if live(1, L + 1):
                    pe.wait_ge(s_yg, i)
                    if upto >= 2:
                        pe.wait_ge(s_x1, i - 1)
                    for b in range(NB):
                        for m in range(KC):
                            last = pe.matmul(bank[5][:, b * D:(b + 1) * D], yg[:, 1 - par, m, b * NJ:(b + 1) * NJ],
                                             w_out_s[:, m, :], start=(m == 0), stop=(m == KC - 1))
                    last.then_inc(s_o, 1)
                if live(3, L + 3):
                    pe.wait_ge(s_xn2, i - 2)
                    if upto >= 5:
                        pe.wait_ge(s_x2s, i - 4)
                    turn(xn, 1 - par, s_xt2)
                if live(4, L + 4):
                    pe.wait_ge(s_x2s, i - 3)
                    for b in range(NB):
                        for k in range(KC):
                            last = pe.matmul(bank67[:, 0, bass.ds(i * (NB * NE) + (b * NE - 4 * NB * NE), NE)],
                                             x2t[:, par, k, b * NJ:(b + 1) * NJ], router_s[:, k, :],
                                             start=(k == 0), stop=(k == KC - 1))
                    last.then_inc(s_lg, 1)

            pe.wait_ge(s_ycs, 2)
            for i in range(6):
                block_b(i, i % 2, i)
            with pe.Fori(3, L // 2 - 1) as q:
                for par in range(2):
                    block_b(q * 2 + par, par)
            for i in range(L - 2, L + 4):
                block_b(i, i % 2, i)

            pe.wait_ge(s_rt, R_COUNT)
            total = count[1][:, NR - 1, :]
            one(bank[0][:, 0:NE], tri[:], total)
            one(bank[1][:, 0:NE], ones[:], total).then_inc(s_cnt, 1)
            for r in range(NR):
                if r % (NR // 2) == 0:
                    pe.wait_ge(s_hot, 1 + r // (NR // 2))
                last = pe.matmul(bank[2][:, 0:NSLOT], lo_hot[:, r, :], slot_r[:, r, :],
                                 start=(r == 0), stop=(r == NR - 1))
            last.then_inc(s_slot, 1)

            def turn_x(t):
                pe.wait_ge(s_xe, t + 1)
                for k in range(KC):
                    for h in range(2):
                        last = pe.transpose(bank[4][:, k * TT + h * P:k * TT + (h + 1) * P],
                                            xe[:, h, k * P:(k + 1) * P], ident[:])
                last.then_inc(s_xet, 1)

            pe.wait_ge(s_ids, 1)
            pe.sem_inc(s_pj, 1)
            turn_x(0)
            with pe.Fori(0, NE // 2) as q:
                for par in range(2):
                    e = q * 2 + par
                    first = pe.value_load(bounds[0:1, bass.ds(e, 1)], min_val=0, max_val=NT - 1)
                    end = pe.value_load(bounds[0:1, bass.ds(e + 1, 1)], min_val=1, max_val=NT)
                    wait_apart(pe, (s_wsp, e + 1), (s_wsd, e + 1))
                    with pe.Fori(first, end) as t:
                        def hidden(c):
                            if c >= 4:
                                pe.wait_ge(s_relu, t * HC + (c - 3))
                            for k in range(KC):
                                w = slice(k * HD + c * P, k * HD + (c + 1) * P)
                                last = three_pass(bank[c % 4][:, 0:TT], (wh[par][:, w], wl[par][:, w]),
                                                  (xe_h[:, k, :], xe_l[:, k, :]), k == 0, k == KC - 1)
                            last.then_inc(s_fc, 1)

                        def project(c):
                            pe.wait_ge(s_sql, t * HC + (c + 1))
                            w = slice(KC * HD + c * D, KC * HD + (c + 1) * D)
                            for h in range(2):
                                tok = slice(h * P, (h + 1) * P)
                                last = three_pass(bank67[:, h, 0:D], (hid_h[:, c, tok], hid_l[:, c, tok]),
                                                  (wh[par][:, w], wl[par][:, w]), c == 0, c == HC - 1)
                            return last

                        pe.wait_ge(s_xel, t + 1)
                        for c in range(4):
                            hidden(c)
                        pe.wait_ge(s_res, t + 1)
                        for c in range(4):
                            project(c)
                            hidden(c + 4)
                        turn_x(t + 1)
                        for c in range(4, HC):
                            last = project(c)
                        last.then_inc(s_pj, 1)

        @block.vector
        def _(dve):
            for q in range(4):
                dve.wait_ge(s_x[q], 16 * NB)
                with dve.Fori(q * QI, (q + 1) * QI) as i:
                    for b in range(NB):
                        last = dve.bn_stats(stats[:, bass.ds(i, 1), b, :].rearrange("p o s -> p (o s)"),
                                            rows[:, b, bass.ds(i, 1), 0:D].rearrange("p o d -> p (o d)"))
                    last.then_inc(s_bn0, 1)
            dve.wait_ge(s_bn0, L)
            dve.tensor_tensor(mean_sum[:], stats[:, :, :, 1], stats[:, :, :, 4], ALU.add).then_inc(s_stat, 1)
            dve.tensor_tensor(mean_dif[:], stats[:, :, :, 1], stats[:, :, :, 4], ALU.subtract).then_inc(s_stat, 1)
            dve.tensor_tensor(var_sum[:], stats[:, :, :, 2], stats[:, :, :, 5], ALU.add).then_inc(s_stat, 1)
            dve.wait_ge(s_stat, 3)
            dve.tensor_scalar(neg_mean[:], mean_sum[:], -0.5, None, ALU.mult).then_inc(s_stat, 1)
            dve.scalar_tensor_tensor(out=mean_dif[:], in0=mean_dif[:], scalar=0.25, in1=mean_dif[:],
                                     op0=ALU.mult, op1=ALU.mult).then_inc(s_stat, 1)
            dve.wait_ge(s_stat, 5)
            dve.scalar_tensor_tensor(out=var[:], in0=var_sum[:], scalar=1.0 / D, in1=mean_dif[:],
                                     op0=ALU.mult, op1=ALU.add).then_inc(s_stat, 1)
            dve.wait_ge(s_std, 1)
            dve.reciprocal(rstd[:], std[:]).then_inc(s_stat, 1)
            dve.wait_ge(s_yc, 1)
            dve.tensor_copy(ycat[0:S, :], bank[3][0:S, 0:D]).then_inc(s_ycs, 1)
            dve.tensor_tensor(ycat[S:2 * S, :], bank[3][S:2 * S, 0:D], d_t_s[S:2 * S, :], ALU.add).then_inc(s_ycs, 1)
            dve.wait_ge(s_stat, 7)

            def norm1(i, par, free):
                if free:
                    dve.wait_ge(s_xt, i - 1)
                for b in range(NB):
                    last = dve.tensor_scalar(xn[:, par, b, :],
                                             rows[:, b, bass.ds(i, 1), 0:D].rearrange("p o d -> p (o d)"),
                                             neg_mean[:, bass.ds(i, 1), b], rstd[:, bass.ds(i, 1), b],
                                             ALU.add, ALU.mult)
                last.then_inc(s_xn, 1)

            def low1(i, par):
                dve.wait_ge(s_xth, i + 1)
                dve.tensor_tensor(xt_l[:, par, :, :].rearrange("p k c -> p (k c)"), bank[par][:, :],
                                  xt_h[:, par, :, :].rearrange("p k c -> p (k c)").bitcast(F32),
                                  ALU.subtract).then_inc(s_xtl, 1)

            norm1(0, 0, False)
            norm1(1, 1, False)
            low1(0, 0)
            norm1(2, 0, True)
            low1(1, 1)
            with dve.Fori(1, L // 2 - 1) as q:
                for par in range(2):
                    i = q * 2 + par
                    norm1(i + 1, 1 - par, True)
                    low1(i, par)
            norm1(L - 1, 1, True)
            low1(L - 2, 0)
            low1(L - 1, 1)

            dve.memset(hu[0:S, 0, 0:1], 0.0)
            dve.memset(hu[0:S, 0, NJ:NJ + 1], 0.0)
            dve.wait_ge(s_e, L)
            dve.tensor_copy(sums_t[:], bank67[:, :, 0:S]).then_inc(s_ecp, 1)
            for b in range(NB):
                dve.wait_ge(s_cmm, b + 1)
                dve.tensor_copy(carry[:, 0, b, :], bank[b][0:S, 0:NJ]).then_inc(s_ccp, 1)
            for r in range(4):
                for b in range(NB):
                    near = carry[:, r % 2, b, :]
                    far = 4 ** r
                    dve.wait_ge(s_ccp, r * NB + b + 1)
                    if r < 3:
                        dst = carry[:, 1 - r % 2, b, :]
                        dve.tensor_copy(dst[:, 0:far], near[:, 0:far])
                    else:
                        dst = hu[0:S, 0, b * NJ + 1:(b + 1) * NJ]
                        near = near[:, 0:NJ - 1]
                        dve.tensor_copy(dst[:, 0:far], near[:, 0:far])
                    dve.wait_ge(s_cmm, (r + 1) * NB + b + 1)
                    width = near.shape[1]
                    dve.tensor_tensor(dst[:, far:width], bank[b][0:S, far:width], near[:, far:width],
                                      ALU.add).then_inc(s_ccp, 1)

            def low_weights(par, nth, piece=0, pieces=1):
                if piece == 0:
                    wait_apart(dve, (s_wsh, nth * 2 + 1))
                c = slice(piece * HALF // pieces, (piece + 1) * HALF // pieces)
                low = dve.tensor_tensor(wl[par][:, c], wraw[:, c], wh[par][:, c].bitcast(F32), ALU.subtract)
                if piece == pieces - 1:
                    low.then_inc(s_wsd, 1)

            def block_b(i, par, upto=4 * L):
                live = lambda lo, hi: upto == 4 * L or lo <= upto < hi
                if live(0, L - 1):
                    dve.wait_ge(s_h, i + 1)
                    dve.tensor_copy(hu[0:S, bass.ds(i + 1, 1), NJ:BC].rearrange("p o c -> p (o c)"),
                                    bank67[0:S, 1, 0:NJ]).then_inc(s_hs1, 1)
                if live(0, L):
                    dve.wait_ge(s_y, i + 1)
                    if upto >= 2:
                        dve.wait_ge(s_o, i - 1)
                    dve.tensor_tensor(yg[:, par, :, :], bank[3 + par][:, :].rearrange("p (m c) -> p m c", m=KC),
                                      gate[:, :, bass.ds(i, 1), :].rearrange("p m o c -> p m (o c)"),
                                      ALU.mult).then_inc(s_yg, 1)
                if live(2, L + 2):
                    dve.wait_ge(s_std2, i - 1)
                    dve.reciprocal(rows[:, :, bass.ds(i - 2, 1), D + 1].rearrange("p b o -> p (b o)"),
                                   std2[:, par, :]).then_inc(s_rc, 1)
                    dve.wait_ge(s_rc, i - 1)
                    if upto >= 4:
                        dve.wait_ge(s_xt2, i - 3)
                    for b in range(NB):
                        row = rows[:, b, bass.ds(i - 2, 1), :].rearrange("p o w -> p (o w)")
                        last = dve.tensor_scalar(xn[:, par, b, :], row[:, 0:D], row[:, D:D + 1],
                                                 row[:, D + 1:D + 2], ALU.add, ALU.mult)
                    last.then_inc(s_xn2, 1)
                if live(1, L + 1):
                    dve.wait_ge(s_o, i)
                    dve.wait_ge(s_bias, i)
                    x1 = rows[:, :, bass.ds(i - 1, 1), 0:D].rearrange("p b o d -> p b (o d)")
                    dve.tensor_tensor(x1, bank[5][:, :].rearrange("p (b d) -> p b d", b=NB), x1,
                                      ALU.add).then_inc(s_x1, 1)
                    wait_apart(dve, (s_x1, i))
                    for b in range(NB):
                        last = dve.bn_stats(stats2[:, 1 - par, b, :],
                                            rows[:, b, bass.ds(i - 1, 1), 0:D].rearrange("p o d -> p (o d)"))
                    last.then_inc(s_bn, 1)
                    wait_apart(dve, (s_bn, i))
                    for b in range(NB):
                        last = dve.bn_aggr(mv2[:, 1 - par, b, :], stats2[:, 1 - par, b, :])
                    last.then_inc(s_mv, 1)
                    dve.wait_ge(s_mv, i)
                    dve.tensor_scalar(rows[:, :, bass.ds(i - 1, 1), D].rearrange("p b o -> p (b o)"),
                                      mv2[:, 1 - par, :, 0], -1.0, None, ALU.mult).then_inc(s_nm, 1)

            for i in range(6):
                block_b(i, i % 2, i)
                if i == 0:
                    low_weights(0, 0)
            with dve.Fori(3, L // 2 - 1) as q:
                for par in range(2):
                    block_b(q * 2 + par, par)
            for i in range(L - 2, L + 2):
                block_b(i, i % 2, i)

            chain = [0]

            def link(ins):
                chain[0] += 1
                ins.then_inc(s_rt, 1)
                dve.wait_ge(s_rt, chain[0])

            def over_e(v):
                return v.unsqueeze(2).to_broadcast([P, NR, NE])

            def over_r(v):
                return v.unsqueeze(1).to_broadcast([P, NR, NE])

            dve.wait_ge(s_lg, L)
            dve.wait_ge(s_const, 9)
            logits = bank67[:, 0, 0:NR * NE].rearrange("p (r e) -> p r e", e=NE)
            link(dve.tensor_reduce(rmax[:], logits, AX_X, ALU.max))
            link(dve.tensor_tensor(prob[:], logits, over_e(rmax[:]), ALU.subtract))
            dve.wait_ge(s_exp, 1)
            link(dve.tensor_reduce(rsum[:], prob[:], AX_X, ALU.add))
            link(dve.reciprocal(rmax[:], rsum[:]))
            link(dve.tensor_tensor(pick[:], prob[:], over_e(rmax[:]), ALU.mult))
            link(dve.tensor_reduce(rsum[:], pick[:], AX_X, ALU.max))
            link(dve.tensor_tensor(prob[:], pick[:], over_e(rsum[:]), ALU.is_equal))
            link(dve.tensor_tensor(pick[:], prob[:], over_r(prefer[:]), ALU.mult))
            link(dve.tensor_reduce(rmax[:], pick[:], AX_X, ALU.max))
            link(dve.tensor_tensor(onehot[:], pick[:], over_e(rmax[:]), ALU.is_equal))
            src = onehot
            for n, far in enumerate((1, 2, 4, 8, 16)):
                dst = count[1 - n % 2]
                dve.tensor_copy(dst[:, 0:far, :], src[:, 0:far, :])
                link(dve.tensor_tensor(dst[:, far:, :], src[:, far:, :], src[:, 0:NR - far, :], ALU.add))
                src = dst
            assert chain[0] == R_COUNT
            dve.wait_ge(s_cnt, 1)
            link(dve.tensor_scalar(tiles_i[:], bank[1][:, 0:NE], float(TT - 1), None, ALU.add))
            link(dve.tensor_single_scalar(pos_i[:, 0:NE], tiles_i[:], TT.bit_length() - 1, ALU.logical_shift_right))
            link(dve.tensor_scalar(tiles[:], pos_i[:, 0:NE], 1.0, None, ALU.max))
            es = tiles
            for n, far in enumerate((1, 2, 4)):
                dst = ends[n % 2]
                dve.tensor_copy(dst[:, 0:far], es[:, 0:far])
                link(dve.tensor_tensor(dst[:, far:], es[:, far:], es[:, 0:NE - far], ALU.add))
                es = dst
            dve.memset(bounds[:, 0:1], 0)
            dve.tensor_copy(bounds[:, 1:NE + 1], es[:])
            link(dve.tensor_tensor(ends[1][:], es[:], tiles[:], ALU.subtract))
            link(dve.scalar_tensor_tensor(out=base[:], in0=ends[1][:], scalar=float(TT), in1=bank[0][:, 0:NE],
                                          op0=ALU.mult, op1=ALU.add))
            link(dve.tensor_tensor(pick[:], src[:], over_r(base[:]), ALU.add))
            link(dve.tensor_tensor(prob[:], pick[:], onehot[:], ALU.mult))
            link(dve.tensor_reduce(rsum[:], prob[:], AX_X, ALU.add))
            link(dve.tensor_scalar(pos_i[:], rsum[:], -1.0, None, ALU.add))
            dve.tensor_single_scalar(lo_i[:], pos_i[:], P - 1, ALU.bitwise_and)
            link(dve.tensor_single_scalar(hi_i[:], pos_i[:], P.bit_length() - 1, ALU.logical_shift_right))
            dve.tensor_copy(lo_f[:], lo_i[:])
            link(dve.tensor_copy(hi_f[:], hi_i[:]))
            link(dve.tensor_tensor(slot_v[:], lane[:, 0:NSLOT].unsqueeze(1).to_broadcast([P, NR, NSLOT]),
                                   hi_f[:].unsqueeze(2).to_broadcast([P, NR, NSLOT]), ALU.is_equal))
            dve.tensor_tensor(slot_r, slot_v, token[:].rearrange("p i b -> p (i b)").unsqueeze(2)
                              .to_broadcast([P, NR, NSLOT]), ALU.mult)
            for n in range(2):
                r = slice(n * NR // 2, (n + 1) * NR // 2)
                dve.tensor_tensor(lo_hot[:, r, :], lane[:].unsqueeze(1).to_broadcast([P, NR // 2, P]),
                                  lo_f[:, r].unsqueeze(2).to_broadcast([P, NR // 2, P]),
                                  ALU.is_equal).then_inc(s_hot, 1)
            dve.wait_ge(s_slot, 1)
            dve.tensor_scalar(ids[:], bank[2][:, 0:NSLOT], float(NTOK), None, ALU.add).then_inc(s_ids, 1)

            def prepare(t):
                dve.wait_ge(s_in, t * 32 + 32)
                dve.tensor_copy(kept[:, bass.ds(t % 2, 1), :, :].rearrange("p o h d -> p (o h) d"),
                                fetched[:, :, 0:D])
                for h in range(2):
                    last = dve.tensor_scalar(xe[:, h, :], fetched[:, h, 0:D], fetched[:, h, D:D + 1],
                                             fetched[:, h, D + 1:D + 2], ALU.add, ALU.mult)
                last.then_inc(s_xe, 1)

            def low_x(t):
                dve.wait_ge(s_xeh, t + 1)
                dve.tensor_tensor(xe_l[:].rearrange("p k c -> p (k c)"), bank[4][:, :],
                                  xe_h[:].rearrange("p k c -> p (k c)").bitcast(F32), ALU.subtract).then_inc(s_xel, 1)

            def expert_bounds(e):
                return (dve.value_load(bounds[0:1, bass.ds(e, 1)], min_val=0, max_val=NT - 1),
                        dve.value_load(bounds[0:1, bass.ds(e + 1, 1)], min_val=1, max_val=NT))

            def tile(t, split=None):
                def low_square(c):
                    dve.wait_ge(s_sqs, t * HC + (c + 1))
                    dve.wait_ge(s_sqh, t * HC + (c + 1))
                    dve.tensor_tensor(hid_l[:, c, :], sq_s[:, c % 4, :], hid_h[:, c, :].bitcast(F32),
                                      ALU.subtract).then_inc(s_sql, 1)

                for c in range(HC):
                    dve.wait_ge(s_relu, t * HC + (c + 1))
                    dve.wait_ge(*((s_sql, t * HC + (c - 3)) if c >= 4 else (s_xel, t + 1)))
                    dve.tensor_tensor(sq_s[:, c % 4, :], relu_s[:, c % 4, :], relu_s[:, c % 4, :],
                                      ALU.mult).then_inc(s_sqs, 1)
                    if c >= 1:
                        low_square(c - 1)
                    if c == 4:
                        dve.wait_ge(s_xet, t + 1)
                        prepare(t + 1)
                    elif split and c >= 3:
                        low_weights(*split, (3, 5, 6, 7).index(c), 4)
                low_square(HC - 1)
                low_x(t + 1)
                dve.wait_ge(s_pj, t + 2)
                dve.wait_ge(s_out, t * 32 + 32)
                dve.tensor_tensor(result, bank67[:, :, 0:D],
                                  kept[:, bass.ds(t % 2, 1), :, :].rearrange("p o h d -> p (o h) d"),
                                  ALU.add).then_inc(s_res, 1)

            def run_tiles(first, end):
                with dve.Fori(first, end) as t:
                    tile(t)

            def run_expert(par, e):
                first, end = expert_bounds(e)
                tile(first, (1 - par, e + 1))
                with dve.If(first + 1 < end):
                    run_tiles(first + 1, end)

            dve.wait_ge(s_ids, 1)
            dve.sem_inc(s_res, 1)
            prepare(0)
            low_x(0)
            with dve.Fori(0, NE // 2 - 1) as q:
                for par in range(2):
                    run_expert(par, q * 2 + par)
            run_expert(0, NE - 2)
            first, end = expert_bounds(NE - 1)
            run_tiles(first, end)


def kernel(**inputs):
    import numpy as _np
    import concourse.bacc as _bacc
    from concourse import mybir as _mybir
    from concourse.bass_utils import run_bass_kernel_spmd as _run

    g = {k: _np.asarray(v) for k, v in inputs.items()}
    fc = g["L0_ffn_expert_fc"]
    pj = g["L0_ffn_expert_proj"]
    ne, d, hd = fc.shape
    lay = {
        "x_in": g["L0_attn_x"],
        "w_in": g["L0_attn_W_in"],
        "b_in": g["L0_attn_b_in"],
        "w_gate": g["L0_attn_W_gate"],
        "b_gate": g["L0_attn_b_gate"],
        "w_out": g["L0_attn_W_out"],
        "b_out": g["L0_attn_b_out"],
        "a_mat": g["L0_attn_A"],
        "ab_t": _np.concatenate([g["L0_attn_A"].T, g["L0_attn_Bm"].T], axis=1),
        "b_mat": g["L0_attn_Bm"],
        "c_t": g["L0_attn_C"].T,
        "d_t": g["L0_attn_D"].T,
        "router_t": g["L0_ffn_router_w"].T,
        "fc": fc.reshape(ne, d // P, P, hd).transpose(0, 2, 1, 3),
        "proj": pj.transpose(0, 2, 1).reshape(ne, hd // P, P, d).transpose(0, 2, 1, 3),
    }
    nc = _bacc.Bacc("TRN2", target_bir_lowering=False, num_devices=1)
    arrays, args = {}, []
    for name, a in lay.items():
        a = _np.ascontiguousarray(a)
        arrays[f"{name}_dram"] = a
        args.append(nc.dram_tensor(f"{name}_dram", a.shape, _mybir.dt.from_np(a.dtype), kind="ExternalInput").ap())
    nb, t, d = lay["x_in"].shape
    args.append(nc.dram_tensor("out_dram", (nb * t, d), _mybir.dt.float32, kind="ExternalOutput").ap())
    ssm_moe_kernel(nc, *args)
    r = _run(nc, [arrays], core_ids=[0])
    return r.results[0]["out_dram"].reshape(nb, t, d)
```

```python
from contextlib import ExitStack

import concourse.bass as bass
from concourse import mybir

ALU = mybir.AluOpType
ACT = mybir.ActivationFunctionType
F32 = mybir.dt.float32
F32R = mybir.dt.float32r
I32 = mybir.dt.int32
U32 = mybir.dt.uint32
AX_X = mybir.AxisListType.X
P = 128


def ssm_moe_kernel(nc, x, w_mix, w_gate, w_out, w_out_t, b_out, bias_cols, a_mat, ab, ab_t, cd_t, place, fc, proj, out):
    NB, T, D = x.shape
    S = a_mat.shape[0]
    NE = fc.shape[0]
    HD = fc.shape[3]
    KC = D // P
    HC = HD // P
    NJ = P
    L = T // NJ
    NR = NB * L
    NTOK = NB * T
    BC = NB * NJ
    CM, CS = D + NE, D + NE + 1
    ROW = D + NE + 2
    TT = 2 * P
    NT = NTOK // TT + NE - 1
    NSLOT = 2 * (NT + 2)
    WC = KC * HD + HC * D
    EPS = 1e-5
    assert NB == 2 and KC == 2 and S == 64 and L == 16 and HC == 8 and NE == 8 and BC == TT

    x_rows = x.rearrange("b (j i) d -> j b i d", i=L)
    scratch = nc.dram_tensor("x1_rows", (NTOK + 1, ROW), F32, kind="Internal").ap()
    scratch_rows = scratch[0:NTOK, :].rearrange("(b j i) w -> j b i w", b=NB, i=L)

    with ExitStack() as ctx:
        def sem(name):
            return ctx.enter_context(nc.semaphore(name))

        def allocator(stack):
            def sb(name, shape, dt=F32):
                return stack.enter_context(nc.sbuf_tensor(name, shape, dt))
            return sb

        sb = allocator(ctx)
        rows = sb("rows", [P, NB, L, ROW])
        gate = sb("gate", [P, KC, L, BC])
        wraw = sb("wraw", [P, WC])
        wh0 = sb("wh0", [P, WC], F32R)
        wl0 = sb("wl0", [P, WC], F32R)
        ident = sb("ident", [P, P])
        ones = sb("ones", [P, P])
        tri = sb("tri", [P, P])
        eps_s = sb("eps_s", [P, 1])
        zero_row = sb("zero_row", [1, ROW])
        lane = sb("lane", [P, P])
        token = sb("token", [P, L, NB])
        prob = sb("prob", [P, NR, NE])
        pick = sb("pick", [P, NR, NE])
        prob2 = sb("prob2", [P, NR, NE])
        onehot = sb("onehot", [P, NR * NE], F32R)
        total_m = sb("total_m", [P, 2, P], F32R)
        place_s = sb("place_s", [P, 2, (NR + 1) * NE])
        place_r = sb("place_r", [P, 2, (NR + 1) * NE], F32R)
        tri_r = sb("tri_r", [P, P], F32R)
        ones_r = sb("ones_r", [P, P], F32R)
        rmax = sb("rmax", [P, NR])
        rsum = sb("rsum", [P, NR])
        prefer = sb("prefer", [P, NE])
        sums_r = sb("sums_r", [P, 2, NE])
        tiles_i = sb("tiles_i", [P, NE], I32)
        ends = [sb(f"ends{n}", [P, 4 + NE]) for n in range(2)]
        bounds = sb("bounds", [P, NE + 1], I32)
        pos_i = sb("pos_i", [P, NR], I32)
        lo_i = sb("lo_i", [P, NR], I32)
        hi_i = sb("hi_i", [P, NR], I32)
        lo_f = sb("lo_f", [P, NR])
        hi_f = sb("hi_f", [P, NR])
        ids = sb("ids", [P, NSLOT], U32)
        id_in = sb("id_in", [P, 2], U32)
        id_out = sb("id_out", [P, 2], U32)
        fetched = sb("fetched", [P, 2, ROW])
        xe_h = sb("xe_h", [P, KC, TT], F32R)
        xe_l = sb("xe_l", [P, KC, TT], F32R)
        gate_cols = gate[:, :, :, :].rearrange("p m i c -> p (m i c)")
        relu_s = gate_cols[:, 0:4 * TT].rearrange("p (n c) -> p n c", n=4)
        sq_s = gate_cols[:, 4 * TT:8 * TT].rearrange("p (n c) -> p n c", n=4)
        kept = gate_cols[:, 8 * TT:12 * TT].rearrange("p (n h d) -> p n h d", n=2, h=2)
        result = gate_cols[:, 12 * TT:14 * TT].rearrange("p (h d) -> p h d", h=2)
        xe = gate_cols[:, 14 * TT:16 * TT].rearrange("p (h d) -> p h d", h=2)

        slot_v = gate_cols[:, 0:NR * NSLOT].rearrange("p (r s) -> p r s", r=NR)

        mixer = ExitStack()
        sb = allocator(mixer)
        hu = sb("hu", [P, L, BC])
        xn = sb("xn", [P, 2, NB, D])
        xt_h = sb("xt_h", [P, 2, KC, BC], F32R)
        xt_l = sb("xt_l", [P, 2, KC, BC], F32R)
        mix = sb("mix", [P, 2, BC])
        yg = sb("yg", [P, 2, KC, BC])
        w_mix_s = sb("w_mix_s", [P, KC, 2 * S])
        w_mix_h = sb("w_mix_h", [P, KC, 2 * S], F32R)
        w_mix_l = sb("w_mix_l", [P, KC, 2 * S], F32R)
        w_gate_s = sb("w_gate_s", [P, KC, D])
        w_gate_h = sb("w_gate_h", [P, KC, D], F32R)
        w_gate_l = sb("w_gate_l", [P, KC, D], F32R)
        w_ext = sb("w_ext", [P, KC, D + NE])
        w_out_t_s = sb("w_out_t_s", [P, KC, D])
        bias_s = sb("bias_s", [P, 1 + 2 * KC])
        b_out_m = sb("b_out_m", [P, KC, P])
        b_out_s = sb("b_out_s", [P, D])
        ab_t_s = sb("ab_t_s", [P, 2 * S])
        cd_t_s = sb("cd_t_s", [P, D])
        ycat = sb("ycat", [P, D])
        step_w = sb("step_w", [P, S])
        powers = sb("powers", [S, L + 1, S])
        pow_t = sb("pow_t", [S, 4, S])
        carry_w = sb("carry_w", [S, 10, S])
        carry_t = sb("carry_t", [S, 5, S])
        chunk_w = sb("chunk_w", [P, L, S])
        router_term = sb("router_term", [P, NR, NE])
        stats = sb("stats", [P, L, NB, 6])
        mean_sum = sb("mean_sum", [P, L, NB])
        mean_dif = sb("mean_dif", [P, L, NB])
        var_sum = sb("var_sum", [P, L, NB])
        neg_mean = sb("neg_mean", [P, L, NB])
        var = sb("var", [P, L, NB])
        std = sb("std", [P, L, NB])
        rstd = sb("rstd", [P, L, NB])
        sums_t = sb("sums_t", [P, NB, S])
        carry = sb("carry", [S, 2, NB, NJ])
        stats2 = sb("stats2", [P, 2, NB, 6])
        mv2 = sb("mv2", [P, 2, NB, 2])
        std2 = sb("std2", [P, 2, NB])
        mixer.close()

        sb = allocator(ctx)
        hid_h = sb("hid_h", [P, HC, TT], F32R)
        hid_l = sb("hid_l", [P, HC, TT], F32R)
        wh1 = sb("wh1", [P, WC], F32R)
        wl1 = sb("wl1", [P, WC], F32R)
        wh, wl = [wh0, wh1], [wl0, wl1]
        token_r = token[:].rearrange("p i b -> p (i b)")
        lo_hot = wh1[:, 0:NR * P].rearrange("p (r c) -> p r c", r=NR)
        slot_r = wl1[:, 0:NR * NSLOT].rearrange("p (r s) -> p r s", r=NR)

        bank01 = ctx.enter_context(nc.psum_tensor("bank01", [P, 2, 512], F32))
        bank = [bank01[:, 0, :], bank01[:, 1, :]]
        bank += [ctx.enter_context(nc.psum_tensor(f"bank{n}", [P, 512], F32)) for n in range(2, 6)]
        bank67 = ctx.enter_context(nc.psum_tensor("bank67", [P, 2, 512], F32))

        s_ab = sem("s_ab")
        s_x = [sem(f"s_xq{n}") for n in range(4)]
        s_wa = sem("s_wa")
        s_wl = sem("s_wl")
        s_rawf = sem("s_rawf")
        s_rawp = sem("s_rawp")
        s_const = sem("s_const")
        s_split = sem("s_split")
        s_pmm = sem("s_pmm")
        s_pcp = sem("s_pcp")
        s_yc = sem("s_yc")
        s_ycs = sem("s_ycs")
        s_bm = sem("s_bm")
        s_hu = sem("s_hu")
        s_rx = sem("s_rx")
        s_rp = sem("s_rp")
        s_bn0 = sem("s_bn0")
        s_stat = sem("s_stat")
        s_std = sem("s_std")
        s_xn = sem("s_xn")
        s_xt = sem("s_xt")
        s_xth = sem("s_xth")
        s_xtl = sem("s_xtl")
        s_u = sem("s_u")
        s_us = sem("s_us")
        s_g = sem("s_g")
        s_gs = sem("s_gs")
        s_e = sem("s_e")
        s_ecp = sem("s_ecp")
        s_cmm = sem("s_cmm")
        s_ccp = sem("s_ccp")
        s_bias = sem("s_bias")
        s_h = sem("s_h")
        s_hs = sem("s_hs")
        s_y = sem("s_y")
        s_yg = sem("s_yg")
        s_o = sem("s_o")
        s_x1 = sem("s_x1")
        s_bn = sem("s_bn")
        s_mv = sem("s_mv")
        s_nm = sem("s_nm")
        s_std2 = sem("s_std2")
        s_rc = sem("s_rc")
        s_st = sem("s_st")
        s_rt = sem("s_rt")
        s_exp = sem("s_exp")
        s_cnt = sem("s_cnt")
        s_tot = sem("s_tot")
        s_pos = sem("s_pos")
        s_hotv = sem("s_hotv")
        s_hot = sem("s_hot")
        s_hotp = sem("s_hotp")
        s_slot = sem("s_slot")
        s_ids = sem("s_ids")
        s_wsh = sem("s_wsh")
        s_wsp = sem("s_wsp")
        s_wsd = sem("s_wsd")
        s_idc = sem("s_idc")
        s_odc = sem("s_odc")
        s_in = sem("s_in")
        s_xe = sem("s_xe")
        s_kept = sem("s_kept")
        s_xet = sem("s_xet")
        s_xeh = sem("s_xeh")
        s_xel = sem("s_xel")
        s_fc = sem("s_fc")
        s_relu = sem("s_relu")
        s_sqh = sem("s_sqh")
        s_sqs = sem("s_sqs")
        s_sql = sem("s_sql")
        s_pj = sem("s_pj")
        s_res = sem("s_res")
        s_out = sem("s_out")

        s_tick = sem("s_tick")

        HOT = [slice(0, 4), slice(4, 8), slice(8, 16), slice(16, 24), slice(24, 32)]

        block = ctx.enter_context(nc.Block())
        QI = L // 4
        EXP_COUNT = 5
        R_COUNT = 13
        ROUTER = rows[:, :, :, :].rearrange("p b i w -> p i b w")[:, :, :, D:D + NE]
        NEG_MEAN2 = rows[:, :, :, :].rearrange("p b i w -> p i b w")[:, :, :, CM]
        RSTD2 = rows[:, :, :, :].rearrange("p b i w -> p i b w")[:, :, :, CS]

        def by_block(v):
            return v.rearrange("p (i b) e -> p i b e", b=NB)

        def all_e(v):
            return v.unsqueeze(3).to_broadcast([P, L, NB, NE])

        def all_rows(v):
            return v.unsqueeze(1).unsqueeze(1).to_broadcast([P, L, NB, NE])

        NWL = 16 * 6
        HALF = WC // 2

        def wait_apart(engine, *waits):
            for s, value in waits:
                engine.wait_ge(s, value)
            engine.sem_inc(s_tick, 1)

        @block.sync
        def _(sp):
            sp.dma_start(ab_t_s[:], ab_t).then_inc(s_ab, 16)
            sp.dma_start(powers[:, L - 1, :], a_mat).then_inc(s_ab, 16)

            def load_x(q):
                for b in range(NB):
                    sp.dma_start(rows[:, b, q * QI:(q + 1) * QI, 0:D],
                                 x_rows[:, b, q * QI:(q + 1) * QI, :]).then_inc(s_x[q], 16)

            load_x(0)
            load_x(1)
            sp.dma_start(w_mix_s[:], w_mix.rearrange("(k p) s -> p k s", p=P)).then_inc(s_wa, 16)
            sp.dma_start(w_gate_s[:], w_gate.rearrange("(k p) s -> p k s", p=P)).then_inc(s_wa, 16)
            sp.dma_start(bias_s[:], bias_cols).then_inc(s_wa, 16)
            load_x(2)
            load_x(3)
            sp.dma_start(cd_t_s[:], cd_t).then_inc(s_wl, 16)
            sp.dma_start(step_w[:], ab).then_inc(s_wl, 16)
            sp.dma_start(w_ext[:, :, 0:D], w_out.rearrange("(k p) s -> p k s", p=P)).then_inc(s_wl, 16)
            sp.dma_start(w_out_t_s[:], w_out_t.rearrange("(k p) s -> p k s", p=P)).then_inc(s_wl, 16)
            sp.dma_start(place_s[:], place).then_inc(s_wl, 16)
            sp.dma_start(b_out_s[:], b_out.rearrange("(o d) -> o d", o=1).to_broadcast([P, D])).then_inc(s_wl, 16)
            sp.dma_start(wraw[:, 0:KC * HD], fc[0].rearrange("p k h -> p (k h)")).then_inc(s_rawf, 16)
            sp.dma_start(wraw[:, KC * HD:], proj[0].rearrange("p k d -> p (k d)")).then_inc(s_rawp, 16)
            for q in range(4):
                sp.wait_ge(s_nm, (q + 1) * QI)
                sp.wait_ge(s_rc, (q + 1) * QI)
                sp.dma_start(scratch_rows[:, :, q * QI:(q + 1) * QI, :],
                             rows[:, :, q * QI:(q + 1) * QI, :]).then_inc(s_st, 16)
            with sp.Fori(0, NE - 1) as e:
                sp.wait_ge(s_wsd, e + 1)
                sp.dma_start(wraw[:, 0:HALF],
                             fc[bass.ds(e + 1, 1)].rearrange("o p k h -> p (o k h)")).then_inc(s_rawf, 16)
                sp.wait_ge(s_wsp, e + 1)
                sp.dma_start(wraw[:, HALF:],
                             proj[bass.ds(e + 1, 1)].rearrange("o p k d -> p (o k d)")).then_inc(s_rawp, 16)

        @block.gpsimd
        def _(pool):
            pool.memset(zero_row[:], 0.0).then_inc(s_const, 1)
            pool.memset(ones[:], 1.0).then_inc(s_const, 1)
            pool.wait_ge(s_const, 2)
            pool.dma_start(scratch[NTOK:NTOK + 1, :], zero_row[:]).then_inc(s_out, 32)
            pool.affine_select(out=ident[:], in_=ones[:], compare_op=ALU.is_equal, fill=0.0, base=0,
                               pattern=[[-1, P]], channel_multiplier=1).then_inc(s_const, 1)
            pool.wait_ge(s_const, 3)
            pool.tensor_copy(powers[:, L, :], ident[0:S, 0:S]).then_inc(s_const, 1)
            pool.memset(eps_s[:], EPS).then_inc(s_const, 1)
            pool.affine_select(out=tri[:], in_=ones[:], compare_op=ALU.is_gt, fill=0.0, base=0,
                               pattern=[[1, P]], channel_multiplier=-1).then_inc(s_const, 1)
            pool.iota(prefer[:], pattern=[[-1, NE]], base=NE, channel_multiplier=0,
                      allow_small_or_imprecise_dtypes=True).then_inc(s_const, 1)
            pool.iota(lane[:], pattern=[[1, P]], base=0, channel_multiplier=0,
                      allow_small_or_imprecise_dtypes=True).then_inc(s_const, 1)
            pool.iota(token[:], pattern=[[1, L], [T, NB]], base=-NTOK, channel_multiplier=L,
                      allow_small_or_imprecise_dtypes=True).then_inc(s_const, 1)

            pool.memset(chunk_w[0:S, :, :], 0.0).then_inc(s_const, 1)

            pool.wait_ge(s_wa, 3 * 16)
            pool.tensor_scalar(w_mix_h[:], w_mix_s[:], 1.0, 0.0, ALU.mult, ALU.add).then_inc(s_split, 1)
            pool.tensor_scalar(w_gate_h[:], w_gate_s[:], 1.0, 0.0, ALU.mult, ALU.add).then_inc(s_split, 1)
            pool.wait_ge(s_split, 2)
            pool.tensor_tensor(w_mix_l[:], w_mix_s[:], w_mix_h[:].bitcast(F32), ALU.subtract).then_inc(s_split, 1)
            pool.tensor_tensor(w_gate_l[:], w_gate_s[:], w_gate_h[:].bitcast(F32), ALU.subtract).then_inc(s_split, 1)
            pool.wait_ge(s_wl, NWL)

            def high_weights(par, nth):
                for n, loaded in enumerate((s_rawf, s_rawp)):
                    wait_apart(pool, (loaded, (nth + 1) * 16))
                    c = slice(n * HALF, (n + 1) * HALF)
                    pool.tensor_scalar(wh[par][:, c], wraw[:, c], 1.0, 0.0, ALU.mult, ALU.add).then_inc(s_wsh, 1)

            def low_weights(par, nth):
                pool.wait_ge(s_wsh, (nth + 1) * 2)
                c = slice(HALF, WC)
                pool.tensor_tensor(wl[par][:, c], wraw[:, c], wh[par][:, c].bitcast(F32),
                                   ALU.subtract).then_inc(s_wsp, 1)

            with pool.Fori(0, L) as i:
                pool.wait_ge(s_xn, i + 1)
                for b in range(NB):
                    row = rows[:, b, bass.ds(i, 1), 0:D].rearrange("p o d -> p (o d)")
                    last = pool.tensor_tensor(row, row, b_out_s[:], ALU.add)
                last.then_inc(s_bias, 1)

            pool.wait_ge(s_ycs, 1)
            pool.wait_ge(s_rx, 1)
            pool.tensor_tensor(by_block(router_term[:]), all_e(neg_mean[:]), all_rows(sums_r[:, 0, :]),
                               ALU.mult).then_inc(s_rp, 1)
            pool.tensor_tensor(ROUTER, ROUTER, all_e(std[:]), ALU.mult).then_inc(s_rp, 1)
            pool.wait_ge(s_rp, 2)
            pool.tensor_tensor(ROUTER, ROUTER, by_block(router_term[:]), ALU.subtract).then_inc(s_rp, 1)
            pool.wait_ge(s_rp, 3)
            pool.tensor_tensor(ROUTER, ROUTER, all_rows(sums_r[:, 1, :]), ALU.add).then_inc(s_rp, 1)

            high_weights(0, 0)
            low_weights(0, 0)
            for dst, src in ((place_r, place_s), (tri_r, tri), (ones_r, ones)):
                pool.tensor_scalar(dst[:], src[:], 1.0, 0.0, ALU.mult, ALU.add).then_inc(s_const, 1)

            pool.wait_ge(s_pos, 1)
            for r in range(HOT[-1].start, NR):
                last = pool.tensor_scalar(lo_hot[:, r, :], lane[:], lo_f[:, r:r + 1], None, ALU.is_equal)
            last.then_inc(s_hotp, 1)

            pool.wait_ge(s_ids, 1)
            pool.wait_ge(s_st, 16 * 4)
            pool.wait_ge(s_out, 32)

            def fetch(t):
                pool.tensor_copy(id_in[:], ids[:, bass.ds(t * 2, 2)]).then_inc(s_idc, 1)
                wait_apart(pool, (s_idc, t + 1))
                for h in range(2):
                    pool.indirect_dma_start(fetched[:, h, :], None, scratch[:, :],
                                            bass.IndirectOffsetOnAxis(ap=id_in[:, h:h + 1], axis=0)) \
                        .then_inc(s_in, 16)

            def store(t):
                pool.tensor_copy(id_out[:], ids[:, bass.ds(t * 2, 2)]).then_inc(s_odc, 1)
                wait_apart(pool, (s_odc, t + 1), (s_res, t + 2))
                for h in range(2):
                    pool.indirect_dma_start(out[:, :], bass.IndirectOffsetOnAxis(ap=id_out[:, h:h + 1], axis=0),
                                            result[:, h, :], None, bounds_check=NTOK - 1, oob_is_err=False) \
                        .then_inc(s_out, 16)

            fetch(0)
            pool.wait_ge(s_kept, 1)
            fetch(1)

            def expert_tiles(e):
                first = pool.value_load(bounds[0:1, bass.ds(e, 1)], min_val=0, max_val=NT - 1)
                end = pool.value_load(bounds[0:1, bass.ds(e + 1, 1)], min_val=1, max_val=NT)
                return first, end

            def ahead(t):
                pool.wait_ge(s_kept, t + 2)
                fetch(t + 2)

            def behind(t):
                pool.wait_ge(s_out, t * 32 + 32)
                store(t)

            def run_tiles(first, end):
                with pool.Fori(first, end) as t:
                    ahead(t)
                    behind(t)

            def run_expert(par, e):
                first, end = expert_tiles(e)
                pool.wait_ge(s_pj, first + 1)
                high_weights(1 - par, e + 1)
                ahead(first)
                low_weights(1 - par, e + 1)
                behind(first)
                with pool.If(first + 1 < end):
                    run_tiles(first + 1, end)

            with pool.Fori(0, NE // 2 - 1) as q:
                for par in range(2):
                    run_expert(par, q * 2 + par)
            run_expert(0, NE - 2)
            first, end = expert_tiles(NE - 1)
            run_tiles(first, end)
            pool.wait_ge(s_out, end * 32 + 32)

        @block.scalar
        def _(act):
            def copies(n, pairs):
                act.wait_ge(s_pmm, n)
                for dst, src in pairs:
                    last = act.copy(dst, src)
                last.then_inc(s_pcp, 1)

            for n, m in enumerate((1, 2, 4, 8)):
                new = bank[5][0:S, 0:m * S]
                pairs = [(powers[:, L - 2 * m:L - m, :].rearrange("p k s -> p (k s)"), new),
                         (pow_t[:, n, :], bank[2][0:S, 0:S])]
                if m == 8:
                    pairs.append((carry_w[:, 0, :], bank[5][0:S, 0:S]))
                copies(n + 1, pairs)

            def std1(half):
                h = slice(half * L // 2, (half + 1) * L // 2)
                act.wait_ge(s_stat, 7 * half + 6)
                act.activation(std[:, h, :], var[:, h, :], ACT.Sqrt, bias=eps_s[:, 0:1]).then_inc(s_std, 1)

            act.wait_ge(s_const, 5)
            std1(0)
            copies(5, [(chunk_w[S:2 * S, n * 8:(n + 1) * 8, :].rearrange("p k s -> p (k s)"),
                        bank67[S:2 * S, n, :]) for n in range(2)])
            act.wait_ge(s_wa, 3 * 16)

            def carry_powers(n):
                r = n // 2
                if n % 2 == 0:
                    copies(6 + n, [(carry_w[:, 3 * r + 1, :], bank[2][0:S, 0:S]),
                                   (carry_t[:, 2 * r, :], bank[2][0:S, 2 * S:3 * S])])
                else:
                    pairs = [(carry_w[:, 3 * r + 2:3 * r + 4, :].rearrange("p k s -> p (k s)"),
                              bank[2][0:S, 0:2 * S])]
                    if r < 2:
                        pairs.append((carry_t[:, 2 * r + 1, :], bank[2][0:S, 2 * S:3 * S]))
                    copies(6 + n, pairs)

            def high1(i, par, free):
                act.wait_ge(s_xt, i + 1)
                if free:
                    act.wait_ge(s_g, i - 1)
                act.copy(xt_h[:, par, :, :].rearrange("p k c -> p (k c)"), bank[par][:, :]).then_inc(s_xth, 1)

            def block_a(i, par, free, more=True):
                act.wait_ge(s_u, i + 1)
                if free:
                    act.wait_ge(s_e, i - 1)
                    act.wait_ge(s_hu, i - 1)
                act.activation(mix[:, par, :], bank[2][:, 0:BC], ACT.Identity, bias=bias_s[:, 0:1]).then_inc(s_us, 1)
                if more:
                    high1(i + 1, 1 - par, free or par == 1)
                act.wait_ge(s_g, i + 1)
                for m in range(KC):
                    last = act.activation(gate[:, m, bass.ds(i, 1), :].rearrange("p o c -> p (o c)"),
                                          bank[3 + par][:, m * BC:(m + 1) * BC], ACT.Sigmoid,
                                          bias=bias_s[:, 1 + m:2 + m])
                last.then_inc(s_gs, 1)

            high1(0, 0, False)
            for i in range(8):
                block_a(i, i % 2, i >= 2)
                if i < 6:
                    carry_powers(i)
                if i == 5:
                    std1(1)
            with act.Fori(4, L // 2 - 1) as q:
                for par in range(2):
                    block_a(q * 2 + par, par, True)
            block_a(L - 2, 0, True)
            block_a(L - 1, 1, True, more=False)

            act.wait_ge(s_e, L)
            act.copy(ROUTER, bank[5][:, 0:NR * NE].rearrange("p (i b e) -> p i b e", b=NB, e=NE)).then_inc(s_rx, 1)
            act.wait_ge(s_yc, 1)
            act.copy(w_ext[:, :, D:D + NE], bank[3][:, D:D + KC * NE].rearrange("p (m e) -> p m e", e=NE))
            act.copy(sums_r[:], bank[3][:, D + KC * NE:D + (KC + 2) * NE].rearrange("p (n e) -> p n e", e=NE))
            act.copy(ycat[:], bank[3][:, 0:D]).then_inc(s_ycs, 1)

            def block_b(i, par, upto=4 * L):
                live = lambda lo, hi: upto == 4 * L or lo <= upto < hi
                if live(0, L - 1):
                    act.wait_ge(s_h, i + 1)
                    act.copy(hu[0:S, bass.ds(i + 1, 1), :].rearrange("p o c -> p (o c)"),
                             bank[2][0:S, 0:BC]).then_inc(s_hs, 1)
                if live(2, L + 2):
                    act.wait_ge(s_mv, i - 1)
                    if upto >= 4:
                        act.wait_ge(s_rc, i - 3)
                    act.activation(std2[:, par, :], mv2[:, par, :, 1], ACT.Sqrt,
                                   bias=eps_s[:, 0:1]).then_inc(s_std2, 1)

            for i in range(4):
                block_b(i, i % 2, i)
            with act.Fori(2, L // 2 - 1) as q:
                for par in range(2):
                    block_b(q * 2 + par, par)
            for i in range(L - 2, L + 2):
                block_b(i, i % 2, i)

            act.wait_ge(s_rt, EXP_COUNT)
            act.activation(prob[:], prob[:], ACT.Exp).then_inc(s_exp, 1)

            def high_x(t):
                act.wait_ge(s_xet, t + 1)
                act.copy(xe_h[:].rearrange("p k c -> p (k c)"), bank[4][:, :]).then_inc(s_xeh, 1)

            act.wait_ge(s_ids, 1)
            high_x(0)
            with act.Fori(0, NE) as e:
                first = act.value_load(bounds[0:1, bass.ds(e, 1)], min_val=0, max_val=NT - 1)
                end = act.value_load(bounds[0:1, bass.ds(e + 1, 1)], min_val=1, max_val=NT)
                with act.Fori(first, end) as t:
                    def square(c):
                        act.wait_ge(s_relu, t * HC + (c + 1))
                        act.activation(hid_h[:, c, :], relu_s[:, c % 4, :], ACT.Square).then_inc(s_sqh, 1)

                    for c in range(HC):
                        act.wait_ge(s_fc, t * HC + (c + 1))
                        if c >= 4:
                            act.wait_ge(s_sqs, t * HC + (c - 3))
                        else:
                            act.wait_ge(s_xel, t + 1)
                        act.activation(relu_s[:, c % 4, :], bank[c % 4][:, 0:TT], ACT.Relu).then_inc(s_relu, 1)
                        if c >= 1:
                            square(c - 1)
                    square(HC - 1)
                    high_x(t + 1)

        @block.tensor
        def _(pe):
            def three_pass(dst, lhs, rhs, start, stop):
                pe.matmul(dst, lhs[1], rhs[0], start=start, stop=False)
                pe.matmul(dst, lhs[0], rhs[1], start=False, stop=False)
                return pe.matmul(dst, lhs[0], rhs[0], start=False, stop=stop)

            def one(dst, lhs, rhs):
                return pe.matmul(dst, lhs, rhs, start=True, stop=True)

            pe.wait_ge(s_ab, 32)
            tr = ab_t_s[0:S, 0:S]
            for n, m in enumerate((1, 2, 4, 8)):
                if n:
                    pe.wait_ge(s_pcp, n)
                one(bank[5][0:S, 0:m * S], tr, powers[:, L - m:L, :].rearrange("p k s -> p (k s)"))
                one(bank[2][0:S, 0:S], powers[:, L - m, :], tr).then_inc(s_pmm, 1)
                tr = pow_t[:, n, :]
            pe.wait_ge(s_pcp, 4)
            pe.wait_ge(s_const, 4)
            for n in range(2):
                last = one(bank67[:, n, :], ab_t_s[0:S, :],
                           powers[:, 1 + 8 * n:9 + 8 * n, :].rearrange("p k s -> p (k s)"))
            last.then_inc(s_pmm, 1)

            def carry_powers(n):
                r = n // 2
                tr = pow_t[:, 3, :] if r == 0 else carry_t[:, 2 * r - 1, :]
                t2 = carry_t[:, 2 * r, :]
                if n:
                    pe.wait_ge(s_pcp, 5 + n)
                if n % 2 == 0:
                    one(bank[2][0:S, 0:S], tr, carry_w[:, 3 * r, :])
                    last = one(bank[2][0:S, 2 * S:3 * S], carry_w[:, 3 * r, :], tr)
                else:
                    last = one(bank[2][0:S, 0:2 * S], t2,
                               carry_w[:, 3 * r:3 * r + 2, :].rearrange("p k s -> p (k s)"))
                    if r < 2:
                        last = one(bank[2][0:S, 2 * S:3 * S], carry_w[:, 3 * r + 1, :], t2)
                last.then_inc(s_pmm, 1)

            def turn(src, par, done):
                for k in range(KC):
                    for b in range(NB):
                        last = pe.transpose(bank[par][:, k * BC + b * NJ:k * BC + (b + 1) * NJ],
                                            src[:, par, b, k * P:(k + 1) * P], ident[:])
                last.then_inc(done, 1)

            def turn_a(i, par, free):
                pe.wait_ge(s_xn, i + 1)
                if free:
                    pe.wait_ge(s_xtl, i - 1)
                turn(xn, par, s_xt)

            def block_a(i, par, nth):
                pe.wait_ge(s_xtl, i + 1)
                xs = lambda k: (xt_h[:, par, k, :], xt_l[:, par, k, :])
                if nth:
                    pe.wait_ge(s_us, i)
                if 1 <= nth <= 6:
                    pe.wait_ge(s_pcp, 5 + nth)
                for k in range(KC):
                    last = three_pass(bank[2][:, 0:BC], (w_mix_h[:, k, :], w_mix_l[:, k, :]), xs(k), k == 0, k == KC - 1)
                last.then_inc(s_u, 1)
                if nth >= 2:
                    pe.wait_ge(s_gs, i - 1)
                for m in range(KC):
                    for k in range(KC):
                        w = (w_gate_h[:, k, m * P:(m + 1) * P], w_gate_l[:, k, m * P:(m + 1) * P])
                        last = three_pass(bank[3 + par][:, m * BC:(m + 1) * BC], w, xs(k), k == 0, k == KC - 1)
                last.then_inc(s_g, 1)
                pe.wait_ge(s_us, i + 1)
                for b in range(NB):
                    one(bank[5][:, bass.ds(i * (NB * NE) + b * NE, NE)],
                        mix[0:NE, par, b * NJ:(b + 1) * NJ], ident[0:NE, 0:NE])
                for b in range(NB):
                    last = pe.matmul(bank67[:, b, 0:S], mix[:, par, b * NJ:(b + 1) * NJ],
                                     chunk_w[:, bass.ds(i, 1), :].rearrange("p o s -> p (o s)"),
                                     start=(nth == 0), stop=(nth == L - 1))
                last.then_inc(s_e, 1)

            pe.wait_ge(s_split, 4)
            turn_a(0, 0, False)
            turn_a(1, 1, False)
            pe.wait_ge(s_pcp, 5)
            pe.wait_ge(s_const, 10)
            for i in range(8):
                if i:
                    turn_a(i + 1, (i + 1) % 2, True)
                block_a(i, i % 2, i)
                if i < 6:
                    carry_powers(i)
            with pe.Fori(4, L // 2 - 1) as q:
                for par in range(2):
                    i = q * 2 + par
                    turn_a(i + 1, 1 - par, True)
                    block_a(i, par, 7)
            turn_a(L - 1, 1, True)
            block_a(L - 2, 0, L - 2)
            block_a(L - 1, 1, L - 1)

            pe.wait_ge(s_wl, NWL)
            pe.wait_ge(s_gs, L)
            pe.wait_ge(s_bm, 1)
            router = [w_mix_s[:, k, 0:NE] for k in range(KC)]
            one(bank[3][:, 0:D], ab_t_s[:], cd_t_s[:])
            stationary = [[w_out_t_s[:, k, m * P:(m + 1) * P] for k in range(KC)] for m in range(KC)]
            stationary += [[ones[:]] * KC, [b_out_m[:, k, :] for k in range(KC)]]
            for n, lhs in enumerate(stationary):
                for k in range(KC):
                    last = pe.matmul(bank[3][:, D + n * NE:D + (n + 1) * NE], lhs[k], router[k],
                                     start=(k == 0), stop=(k == KC - 1))
            last.then_inc(s_yc, 1)

            pe.wait_ge(s_ecp, 1)
            for b in range(NB):
                pe.transpose(bank[b][0:S, 0:NJ], sums_t[:, b, :], ident[:]).then_inc(s_cmm, 1)
            for r in range(4):
                terms = range(1, 4 if r < 3 else 2)
                for b in range(NB):
                    pe.wait_ge(s_ccp, r * NB + b + 1)
                    for k in terms:
                        far = k * 4 ** r
                        last = pe.matmul(bank[b][0:S, far:NJ], carry_w[:, 3 * r + k - 1, :],
                                         carry[:, r % 2, b, 0:NJ - far], start=(k == 1), stop=(k == terms[-1]))
                    last.then_inc(s_cmm, 1)

            def block_b(i, par, upto=4 * L):
                live = lambda lo, hi: upto == 4 * L or lo <= upto < hi
                if live(0, L - 1):
                    if upto == 0:
                        pe.wait_ge(s_ccp, 5 * NB)
                    else:
                        pe.wait_ge(s_hs, i)
                    one(bank[2][0:S, 0:BC], step_w[:],
                        hu[:, bass.ds(i, 1), :].rearrange("p o c -> p (o c)")).then_inc(s_h, 1)
                if live(0, L):
                    if upto == L - 1:
                        pe.wait_ge(s_hs, i)
                    if upto >= 2:
                        pe.wait_ge(s_yg, i - 1)
                    for m in range(KC):
                        last = one(bank[3 + par][:, m * BC:(m + 1) * BC], ycat[:, m * P:(m + 1) * P],
                                   hu[:, bass.ds(i, 1), :].rearrange("p o c -> p (o c)"))
                    last.then_inc(s_y, 1)
                if live(1, L + 1):
                    pe.wait_ge(s_yg, i)
                    if upto >= 2:
                        pe.wait_ge(s_x1, i - 1)
                    for b in range(NB):
                        for m in range(KC):
                            last = pe.matmul(bank01[:, b, 0:D + NE], yg[:, 1 - par, m, b * NJ:(b + 1) * NJ],
                                             w_ext[:, m, :], start=(m == 0), stop=(m == KC - 1))
                    last.then_inc(s_o, 1)

            pe.wait_ge(s_ycs, 1)
            for i in range(4):
                block_b(i, i % 2, i)
            with pe.Fori(2, L // 2 - 1) as q:
                for par in range(2):
                    block_b(q * 2 + par, par)
            for i in range(L - 2, L + 1):
                block_b(i, i % 2, i)

            pe.wait_ge(s_const, 13)
            pe.wait_ge(s_rt, R_COUNT)
            for h in range(2):
                last = one(bank[0][:, 2 * h:2 * h + 2], onehot[:, h * P:(h + 1) * P], ones_r[:, 0:2])
            last.then_inc(s_cnt, 1)
            pe.wait_ge(s_tot, 1)
            for h in range(2):
                pe.matmul(bank[1][:, 0:(NR + 1) * NE], total_m[:, h, :], place_r[:, h, :], start=(h == 0), stop=False)
            pe.matmul(bank[1][:, 0:NR * NE], tri_r[:], onehot[:], start=False, stop=True).then_inc(s_cnt, 1)
            for r in range(NR):
                for n, step in enumerate(HOT):
                    if r == step.start:
                        pe.wait_ge(s_hot, n + 1)
                if r == HOT[-1].start:
                    pe.wait_ge(s_hotp, 1)
                last = pe.matmul(bank[2][:, 0:NSLOT], lo_hot[:, r, :], slot_r[:, r, :],
                                 start=(r == 0), stop=(r == NR - 1))
            last.then_inc(s_slot, 1)

            def turn_x(t):
                pe.wait_ge(s_xe, t + 1)
                for k in range(KC):
                    for h in range(2):
                        last = pe.transpose(bank[4][:, k * TT + h * P:k * TT + (h + 1) * P],
                                            xe[:, h, k * P:(k + 1) * P], ident[:])
                last.then_inc(s_xet, 1)

            pe.wait_ge(s_ids, 1)
            pe.sem_inc(s_pj, 1)
            turn_x(0)
            with pe.Fori(0, NE // 2) as q:
                for par in range(2):
                    e = q * 2 + par
                    first = pe.value_load(bounds[0:1, bass.ds(e, 1)], min_val=0, max_val=NT - 1)
                    end = pe.value_load(bounds[0:1, bass.ds(e + 1, 1)], min_val=1, max_val=NT)
                    wait_apart(pe, (s_wsp, e + 1), (s_wsd, e + 1))
                    with pe.Fori(first, end) as t:
                        def hidden(c):
                            if c >= 4:
                                pe.wait_ge(s_relu, t * HC + (c - 3))
                            for k in range(KC):
                                w = slice(k * HD + c * P, k * HD + (c + 1) * P)
                                last = three_pass(bank[c % 4][:, 0:TT], (wh[par][:, w], wl[par][:, w]),
                                                  (xe_h[:, k, :], xe_l[:, k, :]), k == 0, k == KC - 1)
                            last.then_inc(s_fc, 1)

                        def project(c):
                            pe.wait_ge(s_sql, t * HC + (c + 1))
                            w = slice(KC * HD + c * D, KC * HD + (c + 1) * D)
                            for h in range(2):
                                tok = slice(h * P, (h + 1) * P)
                                last = three_pass(bank67[:, h, 0:D], (hid_h[:, c, tok], hid_l[:, c, tok]),
                                                  (wh[par][:, w], wl[par][:, w]), c == 0, c == HC - 1)
                            return last

                        pe.wait_ge(s_xel, t + 1)
                        for c in range(4):
                            hidden(c)
                        pe.wait_ge(s_res, t + 1)
                        for c in range(4):
                            project(c)
                            hidden(c + 4)
                        turn_x(t + 1)
                        for c in range(4, HC):
                            last = project(c)
                        last.then_inc(s_pj, 1)

        @block.vector
        def _(dve):
            def statistics(i):
                for b in range(NB):
                    last = dve.bn_stats(stats[:, bass.ds(i, 1), b, :].rearrange("p o s -> p (o s)"),
                                        rows[:, b, bass.ds(i, 1), 0:D].rearrange("p o d -> p (o d)"))
                last.then_inc(s_bn0, 1)

            def variance(half):
                h = slice(half * L // 2, (half + 1) * L // 2)
                st, done = stats[:, h, :, :], 7 * half
                dve.wait_ge(s_bn0, (half + 1) * L // 2)
                dve.tensor_tensor(mean_sum[:, h, :], st[:, :, :, 1], st[:, :, :, 4], ALU.add).then_inc(s_stat, 1)
                dve.tensor_tensor(mean_dif[:, h, :], st[:, :, :, 1], st[:, :, :, 4], ALU.subtract).then_inc(s_stat, 1)
                dve.tensor_tensor(var_sum[:, h, :], st[:, :, :, 2], st[:, :, :, 5], ALU.add).then_inc(s_stat, 1)
                dve.wait_ge(s_stat, done + 3)
                dve.tensor_scalar(neg_mean[:, h, :], mean_sum[:, h, :], -0.5, None, ALU.mult).then_inc(s_stat, 1)
                dve.scalar_tensor_tensor(out=mean_dif[:, h, :], in0=mean_dif[:, h, :], scalar=0.25,
                                         in1=mean_dif[:, h, :], op0=ALU.mult, op1=ALU.mult).then_inc(s_stat, 1)
                dve.wait_ge(s_stat, done + 5)
                dve.scalar_tensor_tensor(out=var[:, h, :], in0=var_sum[:, h, :], scalar=1.0 / D,
                                         in1=mean_dif[:, h, :], op0=ALU.mult, op1=ALU.add).then_inc(s_stat, 1)

            def inverse(half):
                h = slice(half * L // 2, (half + 1) * L // 2)
                dve.wait_ge(s_std, half + 1)
                dve.reciprocal(rstd[:, h, :], std[:, h, :]).then_inc(s_stat, 1)
                dve.wait_ge(s_stat, 7 * half + 7)

            for q in range(2):
                dve.wait_ge(s_x[q], 16 * NB)
                with dve.Fori(q * QI // 2, (q + 1) * QI // 2) as n:
                    statistics(n * 2)
                    statistics(n * 2 + 1)
            variance(0)
            inverse(0)

            def norm1(i, par, free):
                if free:
                    dve.wait_ge(s_xt, i - 1)
                for b in range(NB):
                    last = dve.tensor_scalar(xn[:, par, b, :],
                                             rows[:, b, bass.ds(i, 1), 0:D].rearrange("p o d -> p (o d)"),
                                             neg_mean[:, bass.ds(i, 1), b], rstd[:, bass.ds(i, 1), b],
                                             ALU.add, ALU.mult)
                last.then_inc(s_xn, 1)

            def low1(i, par):
                dve.wait_ge(s_xth, i + 1)
                dve.tensor_tensor(xt_l[:, par, :, :].rearrange("p k c -> p (k c)"), bank[par][:, :],
                                  xt_h[:, par, :, :].rearrange("p k c -> p (k c)").bitcast(F32),
                                  ALU.subtract).then_inc(s_xtl, 1)

            def place_u(i, par):
                dve.wait_ge(s_us, i + 1)
                dve.tensor_copy(hu[S:2 * S, bass.ds(i, 1), :].rearrange("p o c -> p (o c)"),
                                mix[S:2 * S, par, :]).then_inc(s_hu, 1)

            norm1(0, 0, False)
            norm1(1, 1, False)
            low1(0, 0)
            for i in range(1, 8):
                norm1(i + 1, (i + 1) % 2, True)
                low1(i, i % 2)
                place_u(i - 1, (i - 1) % 2)
                if i <= 4:
                    if i % 2:
                        dve.wait_ge(s_x[2 + i // 2], 16 * NB)
                    statistics(L // 2 + 2 * i - 2)
                    statistics(L // 2 + 2 * i - 1)
                elif i == 5:
                    variance(1)
                elif i == 6:
                    inverse(1)
            with dve.Fori(4, L // 2 - 1) as q:
                for par in range(2):
                    i = q * 2 + par
                    norm1(i + 1, 1 - par, True)
                    low1(i, par)
                    place_u(i - 1, 1 - par)
            norm1(L - 1, 1, True)
            low1(L - 2, 0)
            place_u(L - 3, 1)
            low1(L - 1, 1)
            place_u(L - 2, 0)
            for k in range(KC):
                last = dve.tensor_scalar(b_out_m[:, k, :], ones[:], bias_s[:, 1 + KC + k:2 + KC + k], None, ALU.mult)
            last.then_inc(s_bm, 1)
            place_u(L - 1, 1)

            dve.memset(hu[0:S, 0, 0:1], 0.0)
            dve.memset(hu[0:S, 0, NJ:NJ + 1], 0.0)
            dve.wait_ge(s_e, L)
            dve.tensor_copy(sums_t[:], bank67[:, :, 0:S]).then_inc(s_ecp, 1)
            for b in range(NB):
                dve.wait_ge(s_cmm, b + 1)
                dve.tensor_copy(carry[:, 0, b, :], bank[b][0:S, 0:NJ]).then_inc(s_ccp, 1)
            for r in range(4):
                for b in range(NB):
                    near = carry[:, r % 2, b, :]
                    far = 4 ** r
                    dve.wait_ge(s_ccp, r * NB + b + 1)
                    if r < 3:
                        dst = carry[:, 1 - r % 2, b, :]
                        dve.tensor_copy(dst[:, 0:far], near[:, 0:far])
                    else:
                        dst = hu[0:S, 0, b * NJ + 1:(b + 1) * NJ]
                        near = near[:, 0:NJ - 1]
                        dve.tensor_copy(dst[:, 0:far], near[:, 0:far])
                    dve.wait_ge(s_cmm, (r + 1) * NB + b + 1)
                    width = near.shape[1]
                    dve.tensor_tensor(dst[:, far:width], bank[b][0:S, far:width], near[:, far:width],
                                      ALU.add).then_inc(s_ccp, 1)

            def low_weights(par, nth, piece=0, pieces=1):
                if piece == 0:
                    wait_apart(dve, (s_wsh, nth * 2 + 1))
                c = slice(piece * HALF // pieces, (piece + 1) * HALF // pieces)
                low = dve.tensor_tensor(wl[par][:, c], wraw[:, c], wh[par][:, c].bitcast(F32), ALU.subtract)
                if piece == pieces - 1:
                    low.then_inc(s_wsd, 1)

            def block_b(i, par, upto=4 * L):
                live = lambda lo, hi: upto == 4 * L or lo <= upto < hi
                if live(0, L):
                    dve.wait_ge(s_y, i + 1)
                    if upto >= 2:
                        dve.wait_ge(s_o, i - 1)
                    dve.tensor_tensor(yg[:, par, :, :], bank[3 + par][:, :].rearrange("p (m c) -> p m c", m=KC),
                                      gate[:, :, bass.ds(i, 1), :].rearrange("p m o c -> p m (o c)"),
                                      ALU.mult).then_inc(s_yg, 1)
                if live(2, L + 2):
                    wait_apart(dve, (s_x1, i - 1))
                    for b in range(NB):
                        last = dve.bn_stats(stats2[:, par, b, :],
                                            rows[:, b, bass.ds(i - 2, 1), 0:D].rearrange("p o d -> p (o d)"))
                    last.then_inc(s_bn, 1)
                if live(3, L + 3):
                    dve.wait_ge(s_std2, i - 2)
                    dve.reciprocal(rows[:, :, bass.ds(i - 3, 1), CS].rearrange("p b o -> p (b o)"),
                                   std2[:, 1 - par, :]).then_inc(s_rc, 1)
                if live(1, L + 1):
                    dve.wait_ge(s_o, i)
                    dve.wait_ge(s_bias, i)
                    if upto == 1:
                        dve.wait_ge(s_rp, 4)
                    x1 = rows[:, :, bass.ds(i - 1, 1), 0:CM].rearrange("p b o d -> p b (o d)")
                    dve.tensor_tensor(x1, bank01[:, :, 0:CM], x1, ALU.add).then_inc(s_x1, 1)
                if live(2, L + 2):
                    wait_apart(dve, (s_bn, i - 1))
                    for b in range(NB):
                        last = dve.bn_aggr(mv2[:, par, b, :], stats2[:, par, b, :])
                    last.then_inc(s_mv, 1)
                    dve.wait_ge(s_mv, i - 1)
                    dve.tensor_scalar(rows[:, :, bass.ds(i - 2, 1), CM].rearrange("p b o -> p (b o)"),
                                      mv2[:, par, :, 0], -1.0, None, ALU.mult).then_inc(s_nm, 1)

            for i in range(4):
                block_b(i, i % 2, i)
                if i == 0:
                    low_weights(0, 0)
            with dve.Fori(2, L // 2 - 1) as q:
                for par in range(2):
                    block_b(q * 2 + par, par)
            for i in range(L - 2, L + 3):
                block_b(i, i % 2, i)

            for n in range(2):
                dve.memset(ends[n][:, 0:4], 0.0)

            chain = [0]

            def link(ins):
                chain[0] += 1
                ins.then_inc(s_rt, 1)
                dve.wait_ge(s_rt, chain[0])

            def over_e(v):
                return v.unsqueeze(2).to_broadcast([P, NR, NE])

            def over_r(v):
                return v.unsqueeze(1).to_broadcast([P, NR, NE])

            dve.wait_ge(s_nm, L)
            dve.wait_ge(s_rc, L)
            dve.wait_ge(s_x1, L)
            dve.wait_ge(s_const, 9)
            logits = prob2[:]
            hot_of = onehot[:].rearrange("p (r e) -> p r e", e=NE)
            link(dve.tensor_tensor(by_block(prob[:]), all_e(NEG_MEAN2), all_rows(sums_r[:, 0, :]), ALU.mult))
            link(dve.tensor_tensor(by_block(pick[:]), ROUTER, by_block(prob[:]), ALU.add))
            link(dve.tensor_tensor(by_block(logits), by_block(pick[:]), all_e(RSTD2), ALU.mult))
            link(dve.tensor_reduce(rmax[:], logits, AX_X, ALU.max))
            link(dve.tensor_tensor(prob[:], logits, over_e(rmax[:]), ALU.subtract))
            dve.wait_ge(s_exp, 1)
            link(dve.tensor_reduce(rsum[:], prob[:], AX_X, ALU.add))
            link(dve.reciprocal(rmax[:], rsum[:]))
            link(dve.tensor_tensor(pick[:], prob[:], over_e(rmax[:]), ALU.mult))
            link(dve.tensor_reduce(rsum[:], pick[:], AX_X, ALU.max))
            link(dve.tensor_tensor(prob[:], pick[:], over_e(rsum[:]), ALU.is_equal))
            link(dve.tensor_tensor(pick[:], prob[:], over_r(prefer[:]), ALU.mult))
            link(dve.tensor_reduce(rmax[:], pick[:], AX_X, ALU.max))
            link(dve.tensor_tensor(hot_of, pick[:], over_e(rmax[:]), ALU.is_equal))
            assert chain[0] == R_COUNT
            dve.wait_ge(s_cnt, 1)
            totals = bank[0][:, 0:4].rearrange("p (h o) -> p h o", o=2)[:, :, 0:1]
            dve.tensor_tensor(total_m[:], totals.to_broadcast([P, 2, P]),
                              ones[:].unsqueeze(1).to_broadcast([P, 2, P]), ALU.mult).then_inc(s_tot, 1)
            dve.wait_ge(s_cnt, 2)
            link(dve.tensor_scalar(tiles_i[:], bank[1][:, NR * NE:(NR + 1) * NE], float(TT - 1), None, ALU.add))
            link(dve.tensor_single_scalar(pos_i[:, 0:NE], tiles_i[:], TT.bit_length() - 1, ALU.logical_shift_right))
            link(dve.tensor_scalar(ends[0][:, 4:], pos_i[:, 0:NE], 1.0, None, ALU.max))
            for n, far in enumerate((1, 2, 4)):
                src, dst = ends[n % 2], ends[1 - n % 2]
                link(dve.tensor_tensor(dst[:, 4:], src[:, 4:], src[:, 4 - far:4 + NE - far], ALU.add))
            dve.tensor_copy(bounds[:], ends[1][:, 3:])
            link(dve.scalar_tensor_tensor(out=pick[:], in0=over_r(ends[1][:, 3:3 + NE]), scalar=float(TT),
                                          in1=bank[1][:, 0:NR * NE].rearrange("p (r e) -> p r e", e=NE),
                                          op0=ALU.mult, op1=ALU.add))
            link(dve.tensor_tensor(prob[:], pick[:], hot_of.bitcast(F32), ALU.mult))
            link(dve.tensor_reduce(rsum[:], prob[:], AX_X, ALU.add))
            link(dve.tensor_copy(pos_i[:], rsum[:]))
            dve.tensor_single_scalar(lo_i[:], pos_i[:], P - 1, ALU.bitwise_and)
            link(dve.tensor_single_scalar(hi_i[:], pos_i[:], P.bit_length() - 1, ALU.logical_shift_right))
            dve.tensor_copy(lo_f[:], lo_i[:])
            dve.tensor_copy(hi_f[:], hi_i[:]).then_inc(s_pos, 1)
            dve.wait_ge(s_pos, 1)
            for n, r in enumerate(HOT):
                shape = [P, r.stop - r.start, NSLOT]
                dve.tensor_tensor(slot_v[:, r, :], lane[:, 0:NSLOT].unsqueeze(1).to_broadcast(shape),
                                  hi_f[:, r].unsqueeze(2).to_broadcast(shape), ALU.is_equal).then_inc(s_hotv, 1)
                if n < len(HOT) - 1:
                    rows_shape = [P, r.stop - r.start, P]
                    dve.tensor_tensor(lo_hot[:, r, :], lane[:].unsqueeze(1).to_broadcast(rows_shape),
                                      lo_f[:, r].unsqueeze(2).to_broadcast(rows_shape), ALU.is_equal)
                dve.wait_ge(s_hotv, n + 1)
                dve.tensor_tensor(slot_r[:, r, :], slot_v[:, r, :], token_r[:, r].unsqueeze(2).to_broadcast(shape),
                                  ALU.mult).then_inc(s_hot, 1)
            dve.wait_ge(s_slot, 1)
            dve.tensor_scalar(ids[:], bank[2][:, 0:NSLOT], float(NTOK), None, ALU.add).then_inc(s_ids, 1)

            def prepare(t):
                dve.wait_ge(s_in, t * 32 + 32)
                for h in range(2):
                    last = dve.tensor_scalar(xe[:, h, :], fetched[:, h, 0:D], fetched[:, h, CM:CM + 1],
                                             fetched[:, h, CS:CS + 1], ALU.add, ALU.mult)
                last.then_inc(s_xe, 1)
                dve.tensor_copy(kept[:, bass.ds(t % 2, 1), :, :].rearrange("p o h d -> p (o h) d"),
                                fetched[:, :, 0:D]).then_inc(s_kept, 1)

            def low_x(t):
                dve.wait_ge(s_xeh, t + 1)
                dve.tensor_tensor(xe_l[:].rearrange("p k c -> p (k c)"), bank[4][:, :],
                                  xe_h[:].rearrange("p k c -> p (k c)").bitcast(F32), ALU.subtract).then_inc(s_xel, 1)

            def expert_bounds(e):
                return (dve.value_load(bounds[0:1, bass.ds(e, 1)], min_val=0, max_val=NT - 1),
                        dve.value_load(bounds[0:1, bass.ds(e + 1, 1)], min_val=1, max_val=NT))

            def tile(t, split=None):
                def low_square(c):
                    dve.wait_ge(s_sqs, t * HC + (c + 1))
                    dve.wait_ge(s_sqh, t * HC + (c + 1))
                    dve.tensor_tensor(hid_l[:, c, :], sq_s[:, c % 4, :], hid_h[:, c, :].bitcast(F32),
                                      ALU.subtract).then_inc(s_sql, 1)

                for c in range(HC):
                    dve.wait_ge(s_relu, t * HC + (c + 1))
                    dve.wait_ge(*((s_sql, t * HC + (c - 3)) if c >= 4 else (s_xel, t + 1)))
                    dve.tensor_tensor(sq_s[:, c % 4, :], relu_s[:, c % 4, :], relu_s[:, c % 4, :],
                                      ALU.mult).then_inc(s_sqs, 1)
                    if c >= 1:
                        low_square(c - 1)
                    if c == 4:
                        dve.wait_ge(s_xet, t + 1)
                        prepare(t + 1)
                    elif split and c >= 3:
                        low_weights(*split, (3, 5, 6, 7).index(c), 4)
                low_square(HC - 1)
                low_x(t + 1)
                dve.wait_ge(s_pj, t + 2)
                dve.wait_ge(s_out, t * 32 + 32)
                dve.tensor_tensor(result, bank67[:, :, 0:D],
                                  kept[:, bass.ds(t % 2, 1), :, :].rearrange("p o h d -> p (o h) d"),
                                  ALU.add).then_inc(s_res, 1)

            def run_tiles(first, end):
                with dve.Fori(first, end) as t:
                    tile(t)

            def run_expert(par, e):
                first, end = expert_bounds(e)
                tile(first, (1 - par, e + 1))
                with dve.If(first + 1 < end):
                    run_tiles(first + 1, end)

            dve.wait_ge(s_ids, 1)
            dve.sem_inc(s_res, 1)
            prepare(0)
            low_x(0)
            with dve.Fori(0, NE // 2 - 1) as q:
                for par in range(2):
                    run_expert(par, q * 2 + par)
            run_expert(0, NE - 2)
            first, end = expert_bounds(NE - 1)
            run_tiles(first, end)


def kernel(**inputs):
    import numpy as _np
    import concourse.bacc as _bacc
    from concourse import mybir as _mybir
    from concourse.bass_utils import run_bass_kernel_spmd as _run

    g = {k: _np.asarray(v) for k, v in inputs.items()}
    fc = g["L0_ffn_expert_fc"]
    pj = g["L0_ffn_expert_proj"]
    ne, d, hd = fc.shape
    w_in, router = g["L0_attn_W_in"], g["L0_ffn_router_w"]
    state = w_in.shape[1]
    gap = _np.zeros((d, state - ne), w_in.dtype)
    b_in, b_gate, b_out = (g["L0_attn_" + n] for n in ("b_in", "b_gate", "b_out"))
    pairs = _np.arange(g["L0_attn_x"].size // d // P * ne)
    same = pairs[:, None] % ne == pairs[None, :] % ne
    place = _np.concatenate([same & (pairs[:, None] // ne < pairs[None, :] // ne), same[:, :ne]], axis=1)
    lay = {
        "x_in": g["L0_attn_x"],
        "w_mix": _np.concatenate([router.T, gap, w_in], axis=1),
        "w_gate": g["L0_attn_W_gate"],
        "w_out": g["L0_attn_W_out"],
        "w_out_t": g["L0_attn_W_out"].T,
        "b_out": b_out,
        "bias_cols": _np.concatenate([_np.concatenate([_np.zeros_like(b_in), b_in])[:, None],
                                      b_gate.reshape(-1, P).T, b_out.reshape(-1, P).T], axis=1),
        "a_mat": g["L0_attn_A"],
        "ab": _np.concatenate([g["L0_attn_A"], g["L0_attn_Bm"]], axis=0),
        "ab_t": _np.block([[g["L0_attn_A"].T, g["L0_attn_Bm"].T],
                           [_np.zeros((state, state), w_in.dtype), _np.eye(state, dtype=w_in.dtype)]]),
        "cd_t": _np.concatenate([g["L0_attn_C"].T, g["L0_attn_D"].T], axis=0),
        "place": place.reshape(-1, P, place.shape[1]).transpose(1, 0, 2).astype(_np.float32),
        "fc": fc.reshape(ne, d // P, P, hd).transpose(0, 2, 1, 3),
        "proj": pj.transpose(0, 2, 1).reshape(ne, hd // P, P, d).transpose(0, 2, 1, 3),
    }
    nc = _bacc.Bacc("TRN2", target_bir_lowering=False, num_devices=1)
    arrays, args = {}, []
    for name, a in lay.items():
        a = _np.ascontiguousarray(a)
        arrays[f"{name}_dram"] = a
        args.append(nc.dram_tensor(f"{name}_dram", a.shape, _mybir.dt.from_np(a.dtype), kind="ExternalInput").ap())
    nb, t, d = lay["x_in"].shape
    args.append(nc.dram_tensor("out_dram", (nb * t, d), _mybir.dt.float32, kind="ExternalOutput").ap())
    ssm_moe_kernel(nc, *args)
    r = _run(nc, [arrays], core_ids=[0])
    return r.results[0]["out_dram"].reshape(nb, t, d)
```
